# Optimizing a Trainium2 kernel written in Bass

```python
import numpy as np
import jax
import jax.numpy as jnp

def _softmax(x, axis=-1):
    return jax.nn.softmax(x, axis=axis)

def _gelu(x):
    return jax.nn.gelu(x, approximate=True)

def _silu(x):
    return jax.nn.silu(x)

def _sigmoid(x):
    return jax.nn.sigmoid(x)

def _layernorm(x, axis=-1, eps=1e-05):
    m = jnp.mean(x, axis=axis, keepdims=True)
    v = jnp.var(x, axis=axis, keepdims=True)
    return (x - m) / jnp.sqrt(v + eps)

def _scatter_add(tgt, idx, src, axis=0):
    return tgt.at[idx].add(src)

def _segment_sum(src, seg, n):
    return jax.ops.segment_sum(src, seg, n)
kernel_name = 'mk_dlrm_tower_d1_rec_r8_d7619b'

def setup_inputs(seed: int=0):
    np.random.seed(seed)
    _w = jnp.asarray

    def _rec_inputs():
        import jax
        import jax.numpy as jnp
        _tk = jax.random.key(seed)
        dense_ctx = jax.random.normal(jax.random.fold_in(_tk, 190), (1024, 16), jnp.float32)
        ids = jnp.stack([jax.random.randint(jax.random.fold_in(_tk, 200 + f), (1024,), 0, v, jnp.int32) for f, v in enumerate([1000, 1250, 1000, 125000, 1250, 125000, 1000, 1250, 1250, 125000, 12500, 12500, 125000, 1250, 125000, 125000, 12500, 1250, 1000, 12500, 12500, 1250, 1000, 1250, 1000, 1250, 1000, 1250, 12500, 1250, 1000, 1250])], axis=1)
        tbl_0 = 0.05 * jax.random.normal(jax.random.fold_in(_tk, 500 + 0), (1000, 16), jnp.float32)
        tbl_1 = 0.05 * jax.random.normal(jax.random.fold_in(_tk, 500 + 1), (1250, 16), jnp.float32)
        tbl_2 = 0.05 * jax.random.normal(jax.random.fold_in(_tk, 500 + 2), (1000, 16), jnp.float32)
        tbl_3 = 0.05 * jax.random.normal(jax.random.fold_in(_tk, 500 + 3), (125000, 16), jnp.float32)
        tbl_4 = 0.05 * jax.random.normal(jax.random.fold_in(_tk, 500 + 4), (1250, 16), jnp.float32)
        tbl_5 = 0.05 * jax.random.normal(jax.random.fold_in(_tk, 500 + 5), (125000, 16), jnp.float32)
        tbl_6 = 0.05 * jax.random.normal(jax.random.fold_in(_tk, 500 + 6), (1000, 16), jnp.float32)
        tbl_7 = 0.05 * jax.random.normal(jax.random.fold_in(_tk, 500 + 7), (1250, 16), jnp.float32)
        tbl_8 = 0.05 * jax.random.normal(jax.random.fold_in(_tk, 500 + 8), (1250, 16), jnp.float32)
        tbl_9 = 0.05 * jax.random.normal(jax.random.fold_in(_tk, 500 + 9), (125000, 16), jnp.float32)
        tbl_10 = 0.05 * jax.random.normal(jax.random.fold_in(_tk, 500 + 10), (12500, 16), jnp.float32)
        tbl_11 = 0.05 * jax.random.normal(jax.random.fold_in(_tk, 500 + 11), (12500, 16), jnp.float32)
        tbl_12 = 0.05 * jax.random.normal(jax.random.fold_in(_tk, 500 + 12), (125000, 16), jnp.float32)
        tbl_13 = 0.05 * jax.random.normal(jax.random.fold_in(_tk, 500 + 13), (1250, 16), jnp.float32)
        tbl_14 = 0.05 * jax.random.normal(jax.random.fold_in(_tk, 500 + 14), (125000, 16), jnp.float32)
        tbl_15 = 0.05 * jax.random.normal(jax.random.fold_in(_tk, 500 + 15), (125000, 16), jnp.float32)
        tbl_16 = 0.05 * jax.random.normal(jax.random.fold_in(_tk, 500 + 16), (12500, 16), jnp.float32)
        tbl_17 = 0.05 * jax.random.normal(jax.random.fold_in(_tk, 500 + 17), (1250, 16), jnp.float32)
        tbl_18 = 0.05 * jax.random.normal(jax.random.fold_in(_tk, 500 + 18), (1000, 16), jnp.float32)
        tbl_19 = 0.05 * jax.random.normal(jax.random.fold_in(_tk, 500 + 19), (12500, 16), jnp.float32)
        tbl_20 = 0.05 * jax.random.normal(jax.random.fold_in(_tk, 500 + 20), (12500, 16), jnp.float32)
        tbl_21 = 0.05 * jax.random.normal(jax.random.fold_in(_tk, 500 + 21), (1250, 16), jnp.float32)
        tbl_22 = 0.05 * jax.random.normal(jax.random.fold_in(_tk, 500 + 22), (1000, 16), jnp.float32)
        tbl_23 = 0.05 * jax.random.normal(jax.random.fold_in(_tk, 500 + 23), (1250, 16), jnp.float32)
        tbl_24 = 0.05 * jax.random.normal(jax.random.fold_in(_tk, 500 + 24), (1000, 16), jnp.float32)
        tbl_25 = 0.05 * jax.random.normal(jax.random.fold_in(_tk, 500 + 25), (1250, 16), jnp.float32)
        tbl_26 = 0.05 * jax.random.normal(jax.random.fold_in(_tk, 500 + 26), (1000, 16), jnp.float32)
        tbl_27 = 0.05 * jax.random.normal(jax.random.fold_in(_tk, 500 + 27), (1250, 16), jnp.float32)
        tbl_28 = 0.05 * jax.random.normal(jax.random.fold_in(_tk, 500 + 28), (12500, 16), jnp.float32)
        tbl_29 = 0.05 * jax.random.normal(jax.random.fold_in(_tk, 500 + 29), (1250, 16), jnp.float32)
        tbl_30 = 0.05 * jax.random.normal(jax.random.fold_in(_tk, 500 + 30), (1000, 16), jnp.float32)
        tbl_31 = 0.05 * jax.random.normal(jax.random.fold_in(_tk, 500 + 31), (1250, 16), jnp.float32)
        _rk = jax.random.fold_in(_tk, 7)
        W_top1 = 0.0693375 * jax.random.normal(jax.random.fold_in(_tk, 801), (208, 512), jnp.float32)
        W_top2 = 0.0441942 * jax.random.normal(jax.random.fold_in(_tk, 802), (512, 256), jnp.float32)
        W_top3 = 0.0625 * jax.random.normal(jax.random.fold_in(_tk, 803), (256, 1), jnp.float32)
        b_top1 = jnp.zeros((512,), jnp.float32)
        b_top2 = jnp.zeros((256,), jnp.float32)
        return (dense_ctx, ids, tbl_0, tbl_1, tbl_2, tbl_3, tbl_4, tbl_5, tbl_6, tbl_7, tbl_8, tbl_9, tbl_10, tbl_11, tbl_12, tbl_13, tbl_14, tbl_15, tbl_16, tbl_17, tbl_18, tbl_19, tbl_20, tbl_21, tbl_22, tbl_23, tbl_24, tbl_25, tbl_26, tbl_27, tbl_28, tbl_29, tbl_30, tbl_31, W_top1, b_top1, W_top2, b_top2, W_top3)
    dense_ctx, ids, tbl_0, tbl_1, tbl_2, tbl_3, tbl_4, tbl_5, tbl_6, tbl_7, tbl_8, tbl_9, tbl_10, tbl_11, tbl_12, tbl_13, tbl_14, tbl_15, tbl_16, tbl_17, tbl_18, tbl_19, tbl_20, tbl_21, tbl_22, tbl_23, tbl_24, tbl_25, tbl_26, tbl_27, tbl_28, tbl_29, tbl_30, tbl_31, W_top1, b_top1, W_top2, b_top2, W_top3 = _rec_inputs()

    def _L0_rec_setup():
        import jax, jax.numpy as jnp
        import numpy as np
        B, M, D = (2048, 32, 16)
        LAYERS = [64, 64, 64]
        key = jax.random.key(seed)
        ks = jax.random.split(key, 4)
        inp = {'embeddings': jax.random.normal(ks[0], (B, M, D), dtype=jnp.float32)}
        hk_1 = M
        for i, hk in enumerate(LAYERS):
            scale = (2.0 / (M * hk_1 + hk)) ** 0.5
            inp[f'W{i}'] = jax.random.normal(ks[i + 1], (M, hk_1, hk), dtype=jnp.float32) * scale
            hk_1 = hk
        return inp
    _L0_rec_all = _L0_rec_setup()
    _L0_rec_in = {k: v for k, v in _L0_rec_all.items() if k in ('W0', 'W1', 'W2')}
    del _L0_rec_all
    return {'dense_ctx': dense_ctx, 'ids': ids, 'tbl_0': tbl_0, 'tbl_1': tbl_1, 'tbl_2': tbl_2, 'tbl_3': tbl_3, 'tbl_4': tbl_4, 'tbl_5': tbl_5, 'tbl_6': tbl_6, 'tbl_7': tbl_7, 'tbl_8': tbl_8, 'tbl_9': tbl_9, 'tbl_10': tbl_10, 'tbl_11': tbl_11, 'tbl_12': tbl_12, 'tbl_13': tbl_13, 'tbl_14': tbl_14, 'tbl_15': tbl_15, 'tbl_16': tbl_16, 'tbl_17': tbl_17, 'tbl_18': tbl_18, 'tbl_19': tbl_19, 'tbl_20': tbl_20, 'tbl_21': tbl_21, 'tbl_22': tbl_22, 'tbl_23': tbl_23, 'tbl_24': tbl_24, 'tbl_25': tbl_25, 'tbl_26': tbl_26, 'tbl_27': tbl_27, 'tbl_28': tbl_28, 'tbl_29': tbl_29, 'tbl_30': tbl_30, 'tbl_31': tbl_31, 'W_top1': W_top1, 'b_top1': b_top1, 'W_top2': W_top2, 'b_top2': b_top2, 'W_top3': W_top3, 'L0_rec_W0': _L0_rec_in['W0'], 'L0_rec_W1': _L0_rec_in['W1'], 'L0_rec_W2': _L0_rec_in['W2']}

def reference(dense_ctx, ids, tbl_0, tbl_1, tbl_2, tbl_3, tbl_4, tbl_5, tbl_6, tbl_7, tbl_8, tbl_9, tbl_10, tbl_11, tbl_12, tbl_13, tbl_14, tbl_15, tbl_16, tbl_17, tbl_18, tbl_19, tbl_20, tbl_21, tbl_22, tbl_23, tbl_24, tbl_25, tbl_26, tbl_27, tbl_28, tbl_29, tbl_30, tbl_31, W_top1, b_top1, W_top2, b_top2, W_top3, L0_rec_W0, L0_rec_W1, L0_rec_W2):
    import jax
    import jax.numpy as jnp

    def _L0_rec_ref(embeddings, W0, W1, W2):
        import jax, jax.numpy as jnp
        import numpy as np
        B, M, D = (2048, 32, 16)
        LAYERS = [64, 64, 64]
        x0 = embeddings
        xk = x0
        outs = []
        for W in (W0, W1, W2):
            xk = jax.nn.relu(jnp.einsum('bmd,bhd,mhk->bkd', x0, xk, W))
            outs.append(jnp.sum(xk, axis=2))
        return jnp.concatenate(outs, axis=1)
    e = jnp.stack([tbl_0[ids[:, 0]], tbl_1[ids[:, 1]], tbl_2[ids[:, 2]], tbl_3[ids[:, 3]], tbl_4[ids[:, 4]], tbl_5[ids[:, 5]], tbl_6[ids[:, 6]], tbl_7[ids[:, 7]], tbl_8[ids[:, 8]], tbl_9[ids[:, 9]], tbl_10[ids[:, 10]], tbl_11[ids[:, 11]], tbl_12[ids[:, 12]], tbl_13[ids[:, 13]], tbl_14[ids[:, 14]], tbl_15[ids[:, 15]], tbl_16[ids[:, 16]], tbl_17[ids[:, 17]], tbl_18[ids[:, 18]], tbl_19[ids[:, 19]], tbl_20[ids[:, 20]], tbl_21[ids[:, 21]], tbl_22[ids[:, 22]], tbl_23[ids[:, 23]], tbl_24[ids[:, 24]], tbl_25[ids[:, 25]], tbl_26[ids[:, 26]], tbl_27[ids[:, 27]], tbl_28[ids[:, 28]], tbl_29[ids[:, 29]], tbl_30[ids[:, 30]], tbl_31[ids[:, 31]]], axis=1)
    z = _L0_rec_ref(e, L0_rec_W0, L0_rec_W1, L0_rec_W2)
    z = z.reshape(z.shape[0], -1)
    h = jnp.concatenate([z, dense_ctx], axis=1)
    h = jnp.maximum(h @ W_top1 + b_top1, 0.0)
    h = jnp.maximum(h @ W_top2 + b_top2, 0.0)
    y = h @ W_top3
    return y

_drawn_inputs = setup_inputs


def setup_inputs(seed=0):
    import zlib

    import numpy as np

    out = dict(_drawn_inputs(seed))
    spreads = {'b_top1': (0.0, 2.0), 'b_top2': (0.0, 0.8)}
    factors = {'tbl_0': 8.0,
     'tbl_1': 8.0,
     'tbl_2': 8.0,
     'tbl_3': 8.0,
     'tbl_4': 8.0,
     'tbl_5': 8.0,
     'tbl_6': 8.0,
     'tbl_7': 8.0,
     'tbl_8': 8.0,
     'tbl_9': 8.0,
     'tbl_10': 8.0,
     'tbl_11': 8.0,
     'tbl_12': 8.0,
     'tbl_13': 8.0,
     'tbl_14': 8.0,
     'tbl_15': 8.0,
     'tbl_16': 8.0,
     'tbl_17': 8.0,
     'tbl_18': 8.0,
     'tbl_19': 8.0,
     'tbl_20': 8.0,
     'tbl_21': 8.0,
     'tbl_22': 8.0,
     'tbl_23': 8.0,
     'tbl_24': 8.0,
     'tbl_25': 8.0,
     'tbl_26': 8.0,
     'tbl_27': 8.0,
     'tbl_28': 8.0,
     'tbl_29': 8.0,
     'tbl_30': 8.0,
     'tbl_31': 8.0,
     'L0_rec_W0': 3.544,
     'L0_rec_W1': 8.0,
     'L0_rec_W2': 8.0,
     'dense_ctx': 7.172}
    for name, (base, spread) in spreads.items():
        noise = np.random.default_rng([zlib.crc32(name.encode()), seed]).standard_normal(out[name].shape)
        drawn = base * np.exp(spread * noise) if base else spread * noise
        out[name] = jnp.asarray(drawn.astype(out[name].dtype))
    for name, factor in factors.items():
        out[name] = (out[name] * factor).astype(out[name].dtype)
    return out
```

```python
from contextlib import ExitStack

import numpy as np

import concourse.bass as bass
from concourse import mybir

F32 = mybir.dt.float32
BF16 = mybir.dt.bfloat16
I32 = mybir.dt.int32
ALU = mybir.AluOpType
ACT = mybir.ActivationFunctionType
AX_X = mybir.AxisListType.X

B, M, D = 1024, 32, 16
H = 64
P = 128
NT = B // P
SIDES, BLOCKS, ROWS = 2, 2, 32
COLS = D * ROWS
WIDE = BLOCKS * COLS
TILES = M * H // P
TILES0 = 16 * M // P
F1, F2 = 512, 256
NCTX = 16
PARTS = 3
ZIN = 3 * H
K3 = H + NCTX
A, Bs = 0, 1

POOL_TILES = (4, 9, 14)
SLOTS, POOL_SLOTS = 3, 2
EARLY = 20

PHASES = [(0, A), (0, Bs), (1, A), (1, Bs), (2, A), (2, Bs)]
STEPS = {0: TILES0, 1: TILES, 2: TILES}


def phase_start(layer, side):
    return sum(STEPS[l] for l, s in PHASES[: PHASES.index((layer, side))])


STEPS_PER_TILE = sum(STEPS[l] for l, _ in PHASES)
DVE_Z_PER_TILE = SIDES * TILES0 * BLOCKS + 4 * (TILES - len(POOL_TILES))
POOL_Z_PER_TILE = 4 * len(POOL_TILES)



def make_units(first, last):
    at = {}

    def put(layer, side, step, units):
        at.setdefault((layer, side, step), []).extend(units)

    for t in range(1, TILES0):
        for s in (A, Bs):
            put(0, s, t - 1, [("rot", s, t, c) for c in range(BLOCKS)])
    put(0, A, TILES0 - 1, [("rot", Bs, 0, c) for c in range(BLOCKS)])
    x0b = [("x0", Bs, t, c) for t in range(TILES) for c in range(BLOCKS)]
    if not first:
        put(1, A, 3, [("h1", 0), ("h1", 1)])
        put(1, A, 7, [("h2",)])
        put(1, A, 11, [("y",)])
    for n, u in enumerate(x0b):
        put(1, A, 2 + n * 14 // len(x0b), [u])
    if not last:
        put(1, Bs, 3, [("T", 0)])
        put(1, Bs, 4, [("T", 1)])
        for n in range(4):
            put(1, Bs, 7 + n, [("rep", n // 2, n % 2)])
        x0a = [("x0", A, t, c) for t in range(TILES) for c in range(BLOCKS)]
        for n, u in enumerate(x0a[:13]):
            put(2, A, 3 + n, [u])
        for n, u in enumerate(x0a[13:]):
            put(2, Bs, 2 + n * 11 // 19, [u])
        put(2, Bs, 13, [("rot", A, 0, c) for c in range(BLOCKS)])
    return at


def events(first, last):
    at = make_units(first, last)
    out = []
    for layer, side in PHASES:
        for step in range(STEPS[layer]):
            out.append(("step", layer, side, step))
            out += [("unit", u) for u in at.get((layer, side, step), [])]
        out.append(("end", layer, side))
    return out


def units_of(first, last):
    return [e[1] for e in events(first, last) if e[0] == "unit"]


PROLOGUE = ([("T", 0), ("T", 1)] + [("rep", n // 2, n % 2) for n in range(4)]
            + [("x0", A, t, c) for t in range(TILES) for c in range(BLOCKS)] + [("rot", A, 0, c) for c in range(BLOCKS)])
EPILOGUE = [("h1", 0), ("h1", 1), ("h2",), ("y",)]


def act_reads(u):
    return u[0] != "rot"


def count_act(units):
    return sum(act_reads(u) for u in units)


UNITS_FIRST, UNITS_TILE, UNITS_LAST = (len(units_of(*x)) for x in ((True, False), (False, False), (False, True)))
ACT_FIRST, ACT_TILE, ACT_LAST = (count_act(units_of(*x)) for x in ((True, False), (False, False), (False, True)))
assert not (len(PROLOGUE) % 2 or UNITS_FIRST % 2 or UNITS_TILE % 2 or UNITS_LAST % 2)


def units_before(i, first):
    return len(PROLOGUE) if first else i * UNITS_TILE + (len(PROLOGUE) + UNITS_FIRST - UNITS_TILE)


def act_units_before(i, first):
    return count_act(PROLOGUE) if first else i * ACT_TILE + (count_act(PROLOGUE) + ACT_FIRST - ACT_TILE)


def dve_steps():
    return [(l, s, t) for l, s in PHASES for t in range(STEPS[l]) if l == 0 or t not in POOL_TILES]


def dve_z_after(layer, side, step, block=1):
    n = 0
    for l, s, t in dve_steps():
        if l == 0:
            if (l, s, t) == (layer, side, step):
                return n + block + 1
            n += BLOCKS
        else:
            n += 1
            if (l, s, t) == (layer, side, step):
                return n


def pool_steps():
    return [(l, s, t) for l, s in PHASES if l for t in POOL_TILES]


def reuse_wait(steps, n, slots, i):
    if n >= slots:
        l, s, t = steps[n - slots]
        return i * STEPS_PER_TILE + phase_start(l, s) + t + 1
    if isinstance(i, int) and i == 0:
        return None
    l, s, t = steps[n - slots]
    return i * STEPS_PER_TILE + (phase_start(l, s) + t + 1 - STEPS_PER_TILE)


def x0a_taken(i, first, t):
    if first:
        return count_act(PROLOGUE[:PROLOGUE.index(("x0", A, t, BLOCKS - 1)) + 1])
    units = units_of(False, False)
    n = count_act(units[:units.index(("x0", A, t, BLOCKS - 1)) + 1])
    return i * ACT_TILE + (act_units_before(0, False) - ACT_TILE + n)


def x0b_taken(i, first, t, units):
    n = count_act(units[:units.index(("x0", Bs, t, BLOCKS - 1)) + 1])
    return act_units_before(i, first) + n


def t1_before(i):
    n = units_of(False, False).index(("T", 1)) + 1
    return i * UNITS_TILE + (units_before(0, False) - UNITS_TILE + n)


RED_PER_TILE = 8
RED_X1 = {A: 1, Bs: 2}
RED_X2 = {A: 3, Bs: 6}
RED_X3A = 5


def build(nc, ids, ctx_t, tables, sel, ident, w0a, w0b, w0d, w1, w2, wt1, bt1, wt2, bt2, wt3, out):
    with ExitStack() as stack:
        def sb(name, shape, dt=F32):
            return stack.enter_context(nc.sbuf_tensor(name, shape, dt))

        def sem(name):
            return stack.enter_context(nc.semaphore(name))

        sel_sb = sb("sel_sb", [PARTS * M, TILES + 1 + TILES0, P], BF16)
        ident_sb = sb("ident_sb", [P, P], BF16)
        w0_sb = sb("w0_sb", [P, TILES0, H])
        w0d_sb = sb("w0d_sb", [2 * M, H])
        w1_sb = sb("w1_sb", [P, TILES, H])
        w2_sb = sb("w2_sb", [P, TILES, H])
        wt1_sb = sb("wt1_sb", [P, 2, F1])
        wt2_sb = sb("wt2_sb", [P, F1 // P, F2])
        wt3_sb = sb("wt3_sb", [P, F2 // P])
        bt1_sb = sb("bt1_sb", [P, F1 // P])
        bt2_sb = sb("bt2_sb", [P, F2 // P])
        ones = sb("ones", [P, 1])
        idx = sb("idx", [P, M], I32)
        emb = sb("emb", [P, M, D])
        parts = sb("parts", [P, D, PARTS, M], BF16)
        x0t = sb("x0t", [PARTS * M, SIDES * WIDE], BF16)
        x0rep = sb("x0rep", [P, SIDES, TILES, WIDE])
        x0four = sb("x0four", [P, SIDES, WIDE])
        squares = sb("squares", [SIDES * M, WIDE])
        xk_copy = sb("xk_copy", [P, SIDES, WIDE])
        z = sb("z", [P, SLOTS, WIDE])
        z_pool = sb("z_pool", [P, POOL_SLOTS, WIDE])
        x3 = sb("x3", [P, COLS])
        in12 = sb("in12", [P, P])
        in3 = sb("in3", [K3, P])
        h1 = sb("h1", [P, F1 // P, P])
        h2 = sb("h2", [P, F2 // P, P])
        y_sb = sb("y_sb", [1, P])
        w0b_sb = z[:, 0, 0:TILES0 * H].rearrange("p (t k) -> p t k", t=TILES0)

        xk = stack.enter_context(nc.psum_tensor("xk", [P, SIDES, WIDE], F32))
        acc = stack.enter_context(nc.psum_tensor("acc", [P, SIDES, COLS], F32))
        stage = stack.enter_context(nc.psum_tensor("stage", [P, 2, COLS], F32))

        const_in = sem("const_in")
        w0_in = sem("w0_in")
        w_in = sem("w_in")
        idx_in = sem("idx_in")
        ctx_in = sem("ctx_in")
        gathered = sem("gathered")
        ones_set = sem("ones_set")
        split = sem("split")
        w0_ready = sem("w0_ready")
        unit_ready = sem("unit_ready")
        unit_taken = sem("unit_taken")
        z_ready = sem("z_ready")
        z_pool_ready = sem("z_pool_ready")
        step_done = sem("step_done")
        xk_ready = sem("xk_ready")
        xk_copied = sem("xk_copied")
        x3_ready = sem("x3_ready")
        reduced = sem("reduced")
        y_out = sem("y_out")

        block = stack.enter_context(nc.Block())

        def over_tiles(eng, body, tail=1):
            body(0, True, False, False)
            with eng.Fori(1, NT - tail) as i:
                body(i, False, False, False)
            for i in range(NT - tail, NT):
                body(i, False, i == NT - 1, i == NT - 2)

        @block.sync
        def _(sp):
            sp.sem_inc(y_out, 16)
            sp.dma_start(idx[:], ids[0:P, :]).then_inc(idx_in, 16)
            sp.dma_start(sel_sb[:], sel).then_inc(const_in, 16)
            sp.dma_start(ident_sb[:], ident).then_inc(const_in, 16)
            sp.dma_start(w0_sb[:], w0a).then_inc(w0_in, 16)
            sp.dma_start(w0b_sb, w0b).then_inc(w0_in, 16)
            for s in range(SIDES):
                sp.dma_start(w0d_sb[s * M:(s + 1) * M, :], w0d).then_inc(w_in, 16)
            sp.dma_start(w1_sb[:], w1).then_inc(w_in, 16)
            sp.dma_start(w2_sb[:], w2).then_inc(w_in, 16)
            sp.dma_start(wt1_sb[:, 0, :], wt1[0:P, :]).then_inc(w_in, 16)
            sp.dma_start(wt1_sb[0:K3, 1, :], wt1[P:P + K3, :]).then_inc(w_in, 16)
            sp.dma_start(wt2_sb[:], wt2.rearrange("(t p) n -> p t n", p=P)).then_inc(w_in, 16)
            sp.dma_start(wt3_sb[:], wt3).then_inc(w_in, 16)
            sp.dma_start(bt1_sb[:], bt1).then_inc(w_in, 16)
            sp.dma_start(bt2_sb[:], bt2).then_inc(w_in, 16)
            sp.wait_ge(gathered, 16 * M)
            sp.dma_start(idx[:], ids[P:2 * P, :]).then_inc(idx_in, 16)

            def body(i, first, last, before_last):
                units = units_of(first, last)
                if not first:
                    sp.wait_ge(unit_ready, units_before(i, first) + (units.index(("h1", 1)) + 1))
                sp.dma_start(in3[H:K3, :], ctx_t[:, bass.ds(i * P, P)]).then_inc(ctx_in, 16)
                if not first:
                    sp.wait_ge(unit_taken, act_units_before(i, first)
                               + count_act(units[:units.index(("y",)) + 1]))
                    sp.dma_start(out[bass.ds(i - 1, 1), :], y_sb[:]).then_inc(y_out, 16)
                if not last and not before_last:
                    sp.wait_ge(gathered, i * (16 * M) + 32 * M)
                    sp.dma_start(idx[:], ids[bass.ds(i * P + 2 * P, P), :]).then_inc(idx_in, 16)

            over_tiles(sp, body, tail=2)
            sp.wait_ge(unit_taken, act_units_before(NT - 1, False) + ACT_LAST + len(EPILOGUE))
            sp.dma_start(out[NT - 1:NT, :], y_sb[:]).then_inc(y_out, 16)
            sp.wait_ge(y_out, 16 * NT + 16)

        @block.gpsimd
        def _(pool):
            def gathers(tables_now):
                for m in tables_now:
                    pool.indirect_dma_start(
                        out=emb[:, m, :], out_offset=None, in_=tables[m],
                        in_offset=bass.IndirectOffsetOnAxis(ap=idx[:, m:m + 1], axis=0),
                    ).then_inc(gathered, 16)

            def split_parts(j):
                one = ones[:, 0:1].unsqueeze(2).to_broadcast([P, M, D])
                part = [parts[:, :, n, :].rearrange("p d m -> p m d") for n in range(PARTS)]
                pool.wait_ge(gathered, j * (16 * M) + 16 * M)
                pool.tensor_mul(part[0], emb[:], one).then_inc(split, 1)
                pool.wait_ge(split, j * 4 + 1)
                pool.tensor_sub(emb[:], emb[:], part[0]).then_inc(split, 1)
                pool.wait_ge(split, j * 4 + 2)
                pool.tensor_mul(part[1], emb[:], one).then_inc(split, 1)
                pool.wait_ge(split, j * 4 + 3)
                pool.tensor_sub(part[2], emb[:], part[1]).then_inc(split, 1)

            pool.memset(ones[:], 1.0).then_inc(ones_set, 1)
            pool.wait_ge(ones_set, 1)
            pool.wait_ge(idx_in, 16)
            gathers(range(M))
            split_parts(0)
            pool.wait_ge(split, 4)
            pool.wait_ge(idx_in, 32)
            gathers(range(EARLY))

            def body(i, first, last, before_last):
                units = units_of(first, last)
                steps = pool_steps()

                def product(n):
                    layer, side, t = steps[n]
                    if layer == 1:
                        if side == A:
                            pool.wait_ge(unit_taken, x0a_taken(i, first, t))
                        else:
                            pool.wait_ge(unit_taken, x0b_taken(i, first, t, units))
                    pool.wait_ge(xk_copied, i * 4 + PHASES.index((layer, side)) - 1)
                    used = reuse_wait(steps, n, POOL_SLOTS, i)
                    if used is not None:
                        pool.wait_ge(step_done, used)
                    pool.tensor_mul(z_pool[:, n % POOL_SLOTS, :], x0rep[:, side, t, :],
                                    xk_copy[:, side, :]).then_inc(z_pool_ready, 1)

                if not last:
                    gathers(range(EARLY, EARLY + 8))
                product(0)
                if not last:
                    gathers(range(EARLY + 8, EARLY + 10))
                product(1)
                if not last:
                    gathers(range(EARLY + 10, M))
                product(2)
                if not last:
                    j = i + 1
                    if first:
                        pool.wait_ge(unit_ready, 2)
                    else:
                        pool.wait_ge(unit_ready, t1_before(i))
                    split_parts(j)
                    if not before_last:
                        pool.wait_ge(split, i * 4 + 8)
                        pool.wait_ge(idx_in, i * 16 + 48)
                done = 0
                for n in range(3, POOL_Z_PER_TILE):
                    product(n)
                    if not last and not before_last:
                        more = EARLY * (n - 2) // (POOL_Z_PER_TILE - 3)
                        gathers(range(done, more))
                        done = more

            over_tiles(pool, body, tail=2)

        @block.tensor
        def _(pe):
            def free_bank(i, units, n, first, prologue=False):
                if prologue:
                    if n >= 2:
                        pe.wait_ge(unit_taken, n - 1)
                    return
                if n < 2:
                    pe.wait_ge(z_ready, i * DVE_Z_PER_TILE + n + 1)
                    return
                u = units[n - 2]
                if act_reads(u):
                    pe.wait_ge(unit_taken, act_units_before(i, first) + count_act(units[:n - 1]))
                else:
                    _, side, t, c = u
                    pe.wait_ge(z_ready, i * DVE_Z_PER_TILE + dve_z_after(0, side, t, c))

            def make(u, n, waits=None):
                bank = stage[:, n % 2, :]
                if u[0] == "T":
                    bank = bank.bitcast(BF16)
                    for k in range(D // 2):
                        d = u[1] * (D // 2) + k
                        last = pe.transpose(bank[0:PARTS * M, k * P:(k + 1) * P],
                                            parts[:, d, :, :].rearrange("p a m -> p (a m)"), ident_sb[:])
                elif u[0] in ("rep", "x0", "rot"):
                    w = {"rep": TILES, "x0": u[2], "rot": TILES + 1 + u[2]}[u[0]]
                    side, c = u[1], u[-1]
                    at = (side * BLOCKS + c) * COLS
                    last = pe.matmul(bank, sel_sb[:, w, :], x0t[:, at:at + COLS], start=True, stop=True)
                elif u[0] == "h1":
                    for m in range(2 * u[1], 2 * u[1] + 2):
                        o = bank[:, (m % 2) * P:(m % 2 + 1) * P]
                        pe.matmul(o, wt1_sb[:, 0, m * P:(m + 1) * P], in12[:], start=True, stop=False)
                        last = pe.matmul(o, wt1_sb[0:K3, 1, m * P:(m + 1) * P], in3[:], start=False, stop=True)
                elif u[0] == "h2":
                    for m in range(F2 // P):
                        for k in range(F1 // P):
                            last = pe.matmul(bank[:, m * P:(m + 1) * P], wt2_sb[:, k, m * P:(m + 1) * P],
                                             h1[:, k, :], start=(k == 0), stop=(k == F1 // P - 1))
                else:
                    for k in range(F2 // P):
                        last = pe.matmul(bank[0:1, 0:P], wt3_sb[:, k:k + 1], h2[:, k, :],
                                         start=(k == 0), stop=(k == F2 // P - 1))
                last.then_inc(unit_ready, 1)

            def mlp_waits(u, i, taken_before):
                if u == ("h1", 0):
                    pe.wait_ge(reduced, i * RED_PER_TILE)
                    pe.wait_ge(ctx_in, i * 16)
                elif u[0] in ("h2", "y"):
                    pe.wait_ge(unit_taken, taken_before)

            pe.wait_ge(const_in, 32)
            for n, u in enumerate(PROLOGUE):
                if u == ("T", 0):
                    pe.wait_ge(split, 4)
                if n == 2:
                    pe.wait_ge(unit_taken, 2)
                free_bank(0, PROLOGUE, n, True, prologue=True)
                make(u, n)
            pe.wait_ge(w0_ready, 1)
            pe.wait_ge(w_in, 16 * 10)

            def body(i, first, last, before_last):
                units = units_of(first, last)
                n = 0
                pool_n = 0
                for e in events(first, last):
                    if e[0] == "unit":
                        u = e[1]
                        if u == ("T", 0):
                            pe.wait_ge(split, i * 4 + 8)
                        if u == ("rep", 0, 0):
                            pe.wait_ge(unit_taken, act_units_before(i, first)
                                       + count_act(units[:units.index(("T", 1)) + 1]))
                        before = {"h1": None, "h2": ("h1", 1), "y": ("h2",)}
                        if u[0] in before:
                            mlp_waits(u, i, act_units_before(i, first)
                                      + (count_act(units[:units.index(before[u[0]]) + 1]) if before[u[0]] else 0))
                        free_bank(i, units, n, first)
                        make(u, n)
                        n += 1
                        continue
                    if e[0] == "end":
                        continue
                    _, layer, side, t = e
                    w = {0: w0_sb, 1: w1_sb, 2: w2_sb}[layer]
                    if layer == 0 and t == 0:
                        if not first:
                            pe.wait_ge(x3_ready, i * 2 + (side - 1))
                        for c in range(BLOCKS):
                            pe.matmul(acc[c * H:(c + 1) * H, side, :], w0d_sb[side * M:(side + 1) * M, :],
                                      squares[side * M:(side + 1) * M, c * COLS:(c + 1) * COLS],
                                      start=True, stop=False)
                    if layer and t in POOL_TILES:
                        src = z_pool[:, pool_n % POOL_SLOTS, :]
                        pool_n += 1
                        pe.wait_ge(z_pool_ready, i * POOL_Z_PER_TILE + pool_n)
                    else:
                        src = z[:, dve_steps().index((layer, side, t)) % SLOTS, :]
                        pe.wait_ge(z_ready, i * DVE_Z_PER_TILE + dve_z_after(layer, side, t))
                    for c in range(BLOCKS):
                        mm = pe.matmul(acc[c * H:(c + 1) * H, side, :], w[:, t, :],
                                       src[:, c * COLS:(c + 1) * COLS],
                                       start=(layer > 0 and t == 0), stop=(t == STEPS[layer] - 1))
                    mm.then_inc(step_done, 1)

            over_tiles(pe, body)
            taken = act_units_before(NT - 1, False) + ACT_LAST
            for n, u in enumerate(EPILOGUE):
                mlp_waits(u, NT, taken + n)
                if n < 2:
                    pe.wait_ge(unit_taken, taken)
                else:
                    pe.wait_ge(unit_taken, taken + n - 1)
                make(u, n)

        @block.scalar
        def _(act):
            def take(u, bank_n, ready, i):
                bank = stage[:, bank_n % 2, :]
                act.wait_ge(unit_ready, ready)
                if u[0] == "T":
                    src = bank.bitcast(BF16)[0:PARTS * M, :].rearrange("p (d q b) -> p d q b", q=SIDES * BLOCKS, b=ROWS)
                    dst = x0t[:, :].rearrange("p (q d b) -> p d q b", q=SIDES * BLOCKS, b=ROWS)
                    half = D // 2
                    op = act.activation(dst[:, u[1] * half:(u[1] + 1) * half], src, ACT.Copy)
                elif u[0] == "rep":
                    _, side, c = u
                    act.activation(x0four[:, side, c * COLS:(c + 1) * COLS], bank, ACT.Copy)
                    op = act.activation(squares[side * M:(side + 1) * M, c * COLS:(c + 1) * COLS],
                                        bank[side * M:(side + 1) * M, :], ACT.Square)
                elif u[0] == "x0":
                    _, side, t, c = u
                    op = act.activation(x0rep[:, side, t, c * COLS:(c + 1) * COLS], bank, ACT.Copy)
                elif u[0] == "h1":
                    for m in range(2 * u[1], 2 * u[1] + 2):
                        op = act.activation(h1[:, m, :], bank[:, (m % 2) * P:(m % 2 + 1) * P], ACT.Relu,
                                            bias=bt1_sb[:, m:m + 1])
                elif u[0] == "h2":
                    for m in range(F2 // P):
                        op = act.activation(h2[:, m, :], bank[:, m * P:(m + 1) * P], ACT.Relu,
                                            bias=bt2_sb[:, m:m + 1])
                else:
                    act.wait_ge(y_out, i * 16)
                    op = act.activation(y_sb[:], bank[0:1, 0:P], ACT.Copy)
                op.then_inc(unit_taken, 1)

            for n, u in enumerate(PROLOGUE):
                if act_reads(u):
                    take(u, n, n + 1, None)

            def body(i, first, last, before_last):
                units = units_of(first, last)
                n = 0
                for e in events(first, last):
                    if e[0] == "unit":
                        u = e[1]
                        if act_reads(u):
                            if u == ("h1", 0):
                                act.wait_ge(w_in, 16 * 10)
                            take(u, n, units_before(i, first) + (n + 1), i)
                        n += 1
                    elif e[0] == "end":
                        _, layer, side = e
                        act.wait_ge(step_done, i * STEPS_PER_TILE + (phase_start(layer, side) + STEPS[layer]))
                        if layer == 2:
                            if side == Bs:
                                act.wait_ge(reduced, i * RED_PER_TILE + RED_X3A)
                            elif not first:
                                act.wait_ge(reduced, i * RED_PER_TILE)
                            act.activation(x3[:], acc[:, side, :], ACT.Relu).then_inc(x3_ready, 1)
                            continue
                        if layer == 1:
                            act.wait_ge(reduced, i * RED_PER_TILE + RED_X1[side])
                        elif not first:
                            act.wait_ge(reduced, i * RED_PER_TILE + (RED_X2[side] - RED_PER_TILE))
                        for c in range(BLOCKS):
                            for half in range(2):
                                op = act.activation(xk[half * H:(half + 1) * H, side, c * COLS:(c + 1) * COLS],
                                                    acc[c * H:(c + 1) * H, side, :], ACT.Relu)
                        op.then_inc(xk_ready, 1)
                        ph = PHASES.index((layer, side)) + 1
                        act.wait_ge(xk_ready, i * 4 + ph)
                        act.activation(xk_copy[:, side, :], xk[:, side, :], ACT.Copy).then_inc(xk_copied, 1)

            over_tiles(act, body)
            for n, u in enumerate(EPILOGUE):
                take(u, n, units_before(NT - 1, False) + UNITS_LAST + n + 1, NT)

        @block.vector
        def _(dve):
            dve.wait_ge(w0_in, 32)
            dve.tensor_add(w0_sb[:, 0:TILES0 - 1, :], w0_sb[:, 0:TILES0 - 1, :], w0b_sb[:, 0:TILES0 - 1, :])
            dve.tensor_add(w0_sb[0:P - M, TILES0 - 1, :], w0_sb[0:P - M, TILES0 - 1, :],
                           w0b_sb[0:P - M, TILES0 - 1, :]).then_inc(w0_ready, 1)
            dve.wait_ge(w0_ready, 1)

            def sum_12(layer, side):
                lo = (layer - 1) * H
                src = xk[lo:lo + H, side, :].rearrange("p (c d b) -> p c b d", c=BLOCKS, d=D)
                dst = in12[lo:lo + H, side * BLOCKS * ROWS:(side + 1) * BLOCKS * ROWS].rearrange(
                    "p (c b) -> p c b", c=BLOCKS)
                dve.tensor_reduce(dst, src, AX_X, ALU.add).then_inc(reduced, 1)

            def sum_3(side, count):
                dve.wait_ge(x3_ready, count)
                for c in range(BLOCKS):
                    at = (side * BLOCKS + c) * ROWS
                    dve.tensor_reduce(in3[0:H, at:at + ROWS],
                                      x3[c * H:(c + 1) * H, :].rearrange("p (d b) -> p b d", d=D),
                                      AX_X, ALU.add).then_inc(reduced, 1)

            def body(i, first, last, before_last):
                units = units_of(first, last)
                for n, (layer, side, t) in enumerate(dve_steps()):
                    used = reuse_wait(dve_steps(), n, SLOTS, i)
                    if used is not None:
                        dve.wait_ge(step_done, used)
                    if layer == 0:
                        for c in range(BLOCKS):
                            u = ("rot", side, t, c)
                            if u[1:3] == (A, 0):
                                ready = units_before(i, first) + (c - 1)
                                bank = c
                            else:
                                ready = units_before(i, first) + (units.index(u) + 1)
                                bank = units.index(u) % 2
                            dve.wait_ge(unit_ready, ready)
                            if t == 0 and c == 0:
                                dve.wait_ge(unit_taken, x0a_taken(i, first, 0))
                            dve.tensor_mul(z[:, n % SLOTS, c * COLS:(c + 1) * COLS], stage[:, bank, :],
                                           x0four[:, side, c * COLS:(c + 1) * COLS]).then_inc(z_ready, 1)
                    else:
                        if layer == 1:
                            if side == A:
                                dve.wait_ge(unit_taken, x0a_taken(i, first, t))
                            else:
                                dve.wait_ge(unit_taken, x0b_taken(i, first, t, units))
                        if t == 0:
                            dve.wait_ge(xk_copied, i * 4 + PHASES.index((layer, side)) - 1)
                        dve.tensor_mul(z[:, n % SLOTS, :], xk[:, side, :], x0rep[:, side, t, :]).then_inc(z_ready, 1)
                    if (layer, side, t) == (0, Bs, 1) and not first:
                        sum_3(Bs, i * 2)
                    if (layer, t) == (1, 10):
                        if side == A and not first:
                            dve.wait_ge(unit_ready, units_before(i, first) + (units.index(("h1", 1)) + 1))
                        sum_12(1, side)
                    if (layer, side, t) == (2, A, 6) or (layer, side, t) == (2, Bs, 8):
                        sum_12(2, side)
                    if (layer, side, t) == (2, Bs, 5):
                        sum_3(A, i * 2 + 1)

            over_tiles(dve, body)
            sum_3(Bs, 2 * NT)


def kernel(**inputs):
    import ml_dtypes
    import concourse.bacc as bacc
    from concourse.bass_utils import run_bass_kernel_spmd

    f = {k: np.asarray(v) for k, v in inputs.items()}
    row = np.arange(M)
    pick = np.zeros((M, TILES + 1 + TILES0, P), np.float32)
    for p in range(P):
        for t in range(TILES):
            pick[2 * t + p // H, t, p] = 1
        pick[p % M, TILES, p] = 1
        for t in range(TILES0):
            pick[(p + 4 * t + p // M + 1) % M, TILES + 1 + t, p] = 1
    sel = np.concatenate([pick] * PARTS).astype(ml_dtypes.bfloat16)
    s = 4 * np.arange(TILES0)[:, None, None] + np.arange(4)[None, :, None] + 1
    there = (row + s) % M
    here = np.broadcast_to(row, there.shape)
    w0 = f["L0_rec_W0"]
    as_w0 = lambda w: np.ascontiguousarray(w.reshape(TILES0, P, H).transpose(1, 0, 2))
    as_w = lambda w: np.ascontiguousarray(w.reshape(TILES, P, H).transpose(1, 0, 2))
    arrays = {
        "ids": f["ids"],
        "ctx_t": np.ascontiguousarray(f["dense_ctx"].T),
        **{f"tbl_{m}": f[f"tbl_{m}"] for m in range(M)},
        "sel": sel,
        "ident": np.eye(P, dtype=ml_dtypes.bfloat16),
        "w0a": as_w0(w0[here, there]),
        "w0b": as_w0(w0[there, here]),
        "w0d": np.ascontiguousarray(w0[row, row]),
        "w1": as_w(f["L0_rec_W1"]),
        "w2": as_w(f["L0_rec_W2"]),
        "wt1": f["W_top1"],
        "bt1": np.ascontiguousarray(f["b_top1"].reshape(F1 // P, P).T),
        "wt2": f["W_top2"],
        "bt2": np.ascontiguousarray(f["b_top2"].reshape(F2 // P, P).T),
        "wt3": np.ascontiguousarray(f["W_top3"].reshape(F2 // P, P).T),
    }
    nc = bacc.Bacc("TRN2", target_bir_lowering=False, num_devices=1)
    ap = {n: nc.dram_tensor(n, a.shape, mybir.dt.from_np(a.dtype), kind="ExternalInput").ap()
          for n, a in arrays.items()}
    out = nc.dram_tensor("y", (NT, P), F32, kind="ExternalOutput").ap()
    build(nc, ap["ids"], ap["ctx_t"], [ap[f"tbl_{m}"] for m in range(M)], ap["sel"], ap["ident"], ap["w0a"],
          ap["w0b"], ap["w0d"], ap["w1"], ap["w2"], ap["wt1"], ap["bt1"], ap["wt2"], ap["bt2"], ap["wt3"], out)
    r = run_bass_kernel_spmd(nc, [arrays], core_ids=[0])
    return r.results[0]["y"].reshape(B, 1)
```

```python
from contextlib import ExitStack

import numpy as np

import concourse.bass as bass
from concourse import mybir

F32 = mybir.dt.float32
BF16 = mybir.dt.bfloat16
I32 = mybir.dt.int32
ALU = mybir.AluOpType
ACT = mybir.ActivationFunctionType
AX_X = mybir.AxisListType.X

B, M, D = 1024, 32, 16
H = 64
P = 128
NT = B // P
SIDES, BLOCKS, ROWS = 2, 2, 32
COLS = D * ROWS
WIDE = BLOCKS * COLS
TILES = M * H // P
TILES0 = 16 * M // P
F1, F2 = 512, 256
NCTX = 16
PARTS = 3
ZIN = 3 * H
K3 = H + NCTX
A, Bs = 0, 1

POOL_TILES = (4, 9, 14)
DMA_TILES = (1, 3, 5, 7, 9, 11, 13, 15)
PE_TILES = [t for t in range(TILES) if t not in DMA_TILES]
COPIES = 4
PITCH = WIDE + 1024 + 64
SLOTS, POOL_SLOTS = 3, 2
EARLY = 20

PHASES = [(0, A), (0, Bs), (1, A), (1, Bs), (2, A), (2, Bs)]
STEPS = {0: TILES0, 1: TILES, 2: TILES}


def phase_start(layer, side):
    return sum(STEPS[l] for l, s in PHASES[: PHASES.index((layer, side))])


STEPS_PER_TILE = sum(STEPS[l] for l, _ in PHASES)
POOL_Z_PER_TILE = 4 * len(POOL_TILES)
DVE_Z_PER_TILE = STEPS_PER_TILE - POOL_Z_PER_TILE
ROTS_PER_TILE = SIDES * TILES0



def pairs(kind, side):
    return [(kind, side, t, c) for t in PE_TILES for c in range(BLOCKS)]


def make_units(first, last):
    at = {}

    def put(units, layer, side, step, per_step, quiet=3):
        steps = [(l, s, t) for l, s in PHASES for t in range(STEPS[l]) if t >= quiet]
        start = steps.index((layer, side, step))
        for n, u in enumerate(units):
            at.setdefault(steps[start + int(n / per_step)], []).append(u)

    if first:
        put(pairs("x0", A)[:4], 0, Bs, TILES0 - 1, 4, quiet=0)
        put(pairs("x0", A)[4:] + pairs("x0", Bs), 1, A, 0, 1.2, quiet=0)
    else:
        put(pairs("x0", Bs), 1, A, 3, 1)
        put([("h1", 0), ("h1", 1)], 1, A, 3, 1)
        put([("h2",)], 1, A, 7, 1)
        put([("y",)], 1, A, 11, 1)
    if not last:
        prepare = [("T", 0), ("T", 1)] + [("rep", s, c) for s in range(SIDES) for c in range(BLOCKS)]
        if first:
            put(prepare, 2, A, 3, 1.5)
            put(pairs("x0_next", A), 2, A, 7, 1)
        else:
            put(prepare, 1, Bs, 10, 1)
            put(pairs("x0_next", A), 2, A, 3, 0.8)
    return at


def events(first, last):
    at = make_units(first, last)
    out = []
    rots = {(A, 0): (A, 2), (A, 1): (A, 3), (A, 2): (Bs, 0), (A, 3): (Bs, 1), (Bs, 0): (Bs, 2), (Bs, 1): (Bs, 3)}
    for layer, side in PHASES:
        for step in range(STEPS[layer]):
            if layer == 0 and (side, step) in rots:
                out.append(("rot", *rots[side, step], False))
            out.append(("step", layer, side, step))
            out += [("unit", u) for u in at.get((layer, side, step), [])]
            if (layer, side, step) == (2, Bs, TILES - 2) and not last:
                out += [("rot", A, 0, True), ("rot", A, 1, True)]
        out.append(("end", layer, side))
    return out


def units_of(first, last):
    return [e[1] for e in events(first, last) if e[0] == "unit"]


PROLOGUE = [("T", 0), ("T", 1)] + [("rep", s, c) for s in range(SIDES) for c in range(BLOCKS)]
EPILOGUE = [("h1", 0), ("h1", 1), ("h2",), ("y",)]
UNITS_FIRST, UNITS_TILE, UNITS_LAST = (len(units_of(*x)) for x in ((True, False), (False, False), (False, True)))
assert not (len(PROLOGUE) % 2 or UNITS_FIRST % 2 or UNITS_TILE % 2 or UNITS_LAST % 2)
assert units_of(True, False)[-BLOCKS * len(PE_TILES):] == units_of(False, False)[-BLOCKS * len(PE_TILES):] == pairs("x0_next", A)


def units_before(i, first):
    return len(PROLOGUE) if first else i * UNITS_TILE + (len(PROLOGUE) + UNITS_FIRST - UNITS_TILE)


def x0_units(i, first, side, t):
    if first or side == Bs:
        return units_before(i, first) + (units_of(first, False).index(("x0", side, t, BLOCKS - 1)) + 1)
    return units_before(i, first) + (BLOCKS * (PE_TILES.index(t) + 1) - BLOCKS * len(PE_TILES))


def dve_steps():
    return [(l, s, t) for l, s in PHASES for t in range(STEPS[l]) if l == 0 or t not in POOL_TILES]


def pool_steps():
    return [(l, s, t) for l, s in PHASES if l for t in POOL_TILES]


def z_after(i, layer, side, t):
    return i * DVE_Z_PER_TILE + (dve_steps().index((layer, side, t)) + 1)


def reuse_wait(steps, n, slots, i):
    l, s, t = steps[n - slots]
    done = phase_start(l, s) + t + 1
    if n >= slots:
        return i * STEPS_PER_TILE + done
    if isinstance(i, int) and i == 0:
        return None
    return i * STEPS_PER_TILE + (done - STEPS_PER_TILE)


RED_PER_TILE = 8
RED_X1 = {A: 1, Bs: 2}
RED_X2 = {A: 3, Bs: 6}
RED_X3A = 5


def build(nc, ids, ctx_t, tables, sel, ident, w0a, w0b, w0d, w1, w2, wt1, bt1, wt2, bt2, wt3, out):
    with ExitStack() as stack:
        def sb(name, shape, dt=F32):
            return stack.enter_context(nc.sbuf_tensor(name, shape, dt))

        def sem(name):
            return stack.enter_context(nc.semaphore(name))

        sel_sb = sb("sel_sb", [PARTS * M, TILES + 1 + TILES0, P], BF16)
        ident_sb = sb("ident_sb", [P, P], BF16)
        w0_sb = sb("w0_sb", [P, TILES0, H])
        w0d_sb = sb("w0d_sb", [2 * M, H])
        w1_sb = sb("w1_sb", [P, TILES, H])
        w2_sb = sb("w2_sb", [P, TILES, H])
        wt1_sb = sb("wt1_sb", [P, 2, F1])
        wt2_sb = sb("wt2_sb", [P, F1 // P, F2])
        wt3_sb = sb("wt3_sb", [P, F2 // P])
        bt1_sb = sb("bt1_sb", [P, F1 // P])
        bt2_sb = sb("bt2_sb", [P, F2 // P])
        ones = sb("ones", [P, 1])
        idx = sb("idx", [P, M], I32)
        emb = sb("emb", [P, M, D])
        parts = sb("parts", [P, D, PARTS, M], BF16)
        x0t = sb("x0t", [PARTS * M, SIDES * WIDE], BF16)
        x0rep = sb("x0rep", [P, SIDES, TILES, WIDE])
        x0four = sb("x0four", [P, SIDES, WIDE])
        squares = sb("squares", [SIDES * M, WIDE])
        xk_copy = sb("xk_copy", [P, SIDES, WIDE])
        z = sb("z", [P, SLOTS, WIDE])
        z_pool = sb("z_pool", [P, POOL_SLOTS, WIDE])
        x3 = sb("x3", [P, COLS])
        in12 = sb("in12", [P, P])
        in3 = sb("in3", [K3, P])
        h1 = sb("h1", [P, F1 // P, P])
        h2 = sb("h2", [P, F2 // P, P])
        y_sb = sb("y_sb", [1, P])
        w0b_sb = z[:, 0, 0:TILES0 * H].rearrange("p (t k) -> p t k", t=TILES0)

        xk = stack.enter_context(nc.psum_tensor("xk", [P, SIDES, WIDE], F32))
        acc = stack.enter_context(nc.psum_tensor("acc", [P, SIDES, COLS], F32))
        stage = stack.enter_context(nc.psum_tensor("stage", [P, 2, COLS], F32))

        const_in = sem("const_in")
        w0_in = sem("w0_in")
        w_in = sem("w_in")
        idx_in = sem("idx_in")
        ctx_in = sem("ctx_in")
        gathered = sem("gathered")
        ones_set = sem("ones_set")
        x0_saved = [sem(f"x0_saved{side}") for side in range(SIDES)]
        x0_loaded = [{t: sem(f"x0_loaded{side}_{t}") for t in DMA_TILES} for side in range(SIDES)]
        split = sem("split")
        w0_ready = sem("w0_ready")
        unit_ready = sem("unit_ready")
        unit_taken = sem("unit_taken")
        rot_ready = sem("rot_ready")
        z_ready = sem("z_ready")
        z_pool_ready = sem("z_pool_ready")
        step_done = sem("step_done")
        xk_ready = sem("xk_ready")
        xk_copied = sem("xk_copied")
        x3_ready = sem("x3_ready")
        reduced = sem("reduced")
        y_out = sem("y_out")

        x0_dram = nc.dram_tensor("x0_dram", (SIDES, COPIES, M, PITCH), F32).ap()

        block = stack.enter_context(nc.Block())

        def wait_x0(eng, i, first, side, t):
            if t in DMA_TILES:
                eng.wait_ge(x0_loaded[side][t], i * 32 + 32)
            else:
                eng.wait_ge(unit_taken, x0_units(i, first, side, t))

        def over_tiles(eng, body, tail=1):
            body(0, True, False, False)
            with eng.Fori(1, NT - tail) as i:
                body(i, False, False, False)
            for i in range(NT - tail, NT):
                body(i, False, i == NT - 1, i == NT - 2)

        @block.sync
        def _(sp):
            sp.sem_inc(y_out, 16)
            sp.dma_start(idx[:], ids[0:P, :]).then_inc(idx_in, 16)
            sp.dma_start(sel_sb[:], sel).then_inc(const_in, 16)
            sp.dma_start(ident_sb[:], ident).then_inc(const_in, 16)
            sp.dma_start(w0_sb[:], w0a).then_inc(w0_in, 16)
            sp.dma_start(w0b_sb, w0b).then_inc(w0_in, 16)
            for s in range(SIDES):
                sp.dma_start(w0d_sb[s * M:(s + 1) * M, :], w0d).then_inc(w_in, 16)
            sp.dma_start(w1_sb[:], w1).then_inc(w_in, 16)
            sp.dma_start(w2_sb[:], w2).then_inc(w_in, 16)
            sp.dma_start(wt1_sb[:, 0, :], wt1[0:P, :]).then_inc(w_in, 16)
            sp.dma_start(wt1_sb[0:K3, 1, :], wt1[P:P + K3, :]).then_inc(w_in, 16)
            sp.dma_start(wt2_sb[:], wt2.rearrange("(t p) n -> p t n", p=P)).then_inc(w_in, 16)
            sp.dma_start(wt3_sb[:], wt3).then_inc(w_in, 16)
            sp.dma_start(bt1_sb[:], bt1).then_inc(w_in, 16)
            sp.dma_start(bt2_sb[:], bt2).then_inc(w_in, 16)
            sp.wait_ge(gathered, 16 * M)
            sp.dma_start(idx[:], ids[P:2 * P, :]).then_inc(idx_in, 16)

            def save_x0(side):
                sp.dma_start(x0_dram[side, :, :, 0:WIDE].rearrange("r m n -> (r m) n"),
                             x0four[:, side, :]).then_inc(x0_saved[side], 16)

            def load_x0(side, t):
                for j in range(P // H):
                    sp.dma_start(x0rep[j * H:(j + 1) * H, side, t, :],
                                 x0_dram[side, :, 2 * t + j, 0:WIDE].unsqueeze(1).to_broadcast(
                                     [COPIES, H // COPIES, WIDE])).then_inc(x0_loaded[side][t], 16)

            sp.wait_ge(unit_taken, len(PROLOGUE))
            for side in range(SIDES):
                save_x0(side)
            for side in range(SIDES):
                sp.wait_ge(x0_saved[side], 16)
                for t in DMA_TILES:
                    load_x0(side, t)

            def body(i, first, last, before_last):
                units = units_of(first, last)
                if not first:
                    sp.wait_ge(unit_ready, units_before(i, first) + (units.index(("h1", 1)) + 1))
                sp.dma_start(in3[H:K3, :], ctx_t[:, bass.ds(i * P, P)]).then_inc(ctx_in, 16)
                if not first:
                    sp.wait_ge(unit_taken, units_before(i, first) + (units.index(("y",)) + 1))
                    sp.dma_start(out[bass.ds(i - 1, 1), :], y_sb[:]).then_inc(y_out, 16)
                if not last and not before_last:
                    sp.wait_ge(gathered, i * (16 * M) + 32 * M)
                    sp.dma_start(idx[:], ids[bass.ds(i * P + 2 * P, P), :]).then_inc(idx_in, 16)

                if not last:
                    def value(v):
                        return v if isinstance(i, int) else sp.to_reg(v)

                    for side in range(SIDES):
                        used = value(i * STEPS_PER_TILE + (phase_start(1, side) + TILES))
                        filled = value(units_before(i, first) + (units.index(("rep", side, 1)) + 1))
                        sp.wait_ge(step_done, used)
                        sp.wait_ge(unit_taken, filled)
                        save_x0(side)
                    for side in range(SIDES):
                        for n, t in enumerate(DMA_TILES):
                            saved = value(i * 16 + 32)
                            used = value(i * STEPS_PER_TILE + (phase_start(2, side) + t + 1))
                            if n == 0:
                                sp.wait_ge(x0_saved[side], saved)
                            sp.wait_ge(step_done, used)
                            load_x0(side, t)

            over_tiles(sp, body, tail=2)
            sp.wait_ge(unit_taken, units_before(NT - 1, False) + UNITS_LAST + len(EPILOGUE))
            sp.dma_start(out[NT - 1:NT, :], y_sb[:]).then_inc(y_out, 16)
            sp.wait_ge(y_out, 16 * NT + 16)

        @block.gpsimd
        def _(pool):
            def gathers(tables_now):
                for m in tables_now:
                    pool.indirect_dma_start(
                        out=emb[:, m, :], out_offset=None, in_=tables[m],
                        in_offset=bass.IndirectOffsetOnAxis(ap=idx[:, m:m + 1], axis=0),
                    ).then_inc(gathered, 16)

            def split_parts(j):
                one = ones[:, 0:1].unsqueeze(2).to_broadcast([P, M, D])
                part = [parts[:, :, n, :].rearrange("p d m -> p m d") for n in range(PARTS)]
                pool.wait_ge(gathered, j * (16 * M) + 16 * M)
                pool.tensor_mul(part[0], emb[:], one).then_inc(split, 1)
                pool.wait_ge(split, j * 4 + 1)
                pool.tensor_sub(emb[:], emb[:], part[0]).then_inc(split, 1)
                pool.wait_ge(split, j * 4 + 2)
                pool.tensor_mul(part[1], emb[:], one).then_inc(split, 1)
                pool.wait_ge(split, j * 4 + 3)
                pool.tensor_sub(part[2], emb[:], part[1]).then_inc(split, 1)

            pool.memset(ones[:], 1.0).then_inc(ones_set, 1)
            pool.wait_ge(ones_set, 1)
            pool.wait_ge(idx_in, 16)
            gathers(range(M))
            split_parts(0)
            pool.wait_ge(split, 4)
            pool.wait_ge(idx_in, 32)
            gathers(range(EARLY))

            def body(i, first, last, before_last):
                units = units_of(first, last)
                steps = pool_steps()

                def product(n):
                    layer, side, t = steps[n]
                    if layer == 1:
                        wait_x0(pool, i, first, side, t)
                    pool.wait_ge(xk_copied, i * 4 + PHASES.index((layer, side)) - 1)
                    used = reuse_wait(steps, n, POOL_SLOTS, i)
                    if used is not None:
                        pool.wait_ge(step_done, used)
                    pool.tensor_mul(z_pool[:, n % POOL_SLOTS, :], x0rep[:, side, t, :],
                                    xk_copy[:, side, :]).then_inc(z_pool_ready, 1)

                if not last:
                    gathers(range(EARLY, EARLY + 8))
                product(0)
                if not last:
                    gathers(range(EARLY + 8, EARLY + 10))
                product(1)
                if not last:
                    gathers(range(EARLY + 10, M))
                product(2)
                if not last:
                    pool.wait_ge(unit_ready, units_before(i, first))
                    split_parts(i + 1)
                    if not before_last:
                        pool.wait_ge(split, i * 4 + 8)
                        pool.wait_ge(idx_in, i * 16 + 48)
                done = 0
                for n in range(3, POOL_Z_PER_TILE):
                    product(n)
                    if not last and not before_last:
                        more = EARLY * (n - 2) // (POOL_Z_PER_TILE - 3)
                        gathers(range(done, more))
                        done = more

            over_tiles(pool, body, tail=2)

        @block.tensor
        def _(pe):
            def spread(dst, w, at):
                for h in range(2):
                    mm = pe.matmul(dst[h * H:(h + 1) * H, :], sel_sb[:, w, h * H:(h + 1) * H],
                                   x0t[:, at:at + COLS], start=True, stop=True)
                return mm

            def make(u, n):
                bank = stage[:, n % 2, :]
                if u[0] == "T":
                    bank = bank.bitcast(BF16)
                    for k in range(D // 2):
                        d = u[1] * (D // 2) + k
                        last = pe.transpose(bank[0:PARTS * M, k * P:(k + 1) * P],
                                            parts[:, d, :, :].rearrange("p a m -> p (a m)"), ident_sb[:])
                elif u[0] in ("rep", "x0", "x0_next"):
                    w = TILES if u[0] == "rep" else u[2]
                    side, c = u[1], u[-1]
                    at = (side * BLOCKS + c) * COLS
                    last = spread(bank, w, at)
                elif u[0] == "h1":
                    for m in range(2 * u[1], 2 * u[1] + 2):
                        o = bank[:, (m % 2) * P:(m % 2 + 1) * P]
                        pe.matmul(o, wt1_sb[:, 0, m * P:(m + 1) * P], in12[:], start=True, stop=False)
                        last = pe.matmul(o, wt1_sb[0:K3, 1, m * P:(m + 1) * P], in3[:], start=False, stop=True)
                elif u[0] == "h2":
                    for m in range(F2 // P):
                        for k in range(F1 // P):
                            last = pe.matmul(bank[:, m * P:(m + 1) * P], wt2_sb[:, k, m * P:(m + 1) * P],
                                             h1[:, k, :], start=(k == 0), stop=(k == F1 // P - 1))
                else:
                    for k in range(F2 // P):
                        last = pe.matmul(bank[0:1, 0:P], wt3_sb[:, k:k + 1], h2[:, k, :],
                                         start=(k == 0), stop=(k == F2 // P - 1))
                last.then_inc(unit_ready, 1)

            def rotate(side, t):
                dst = stage if t % 2 else xk[:, side, :].rearrange("p (c n) -> p c n", c=BLOCKS)
                for c in range(BLOCKS):
                    at = (side * BLOCKS + c) * COLS
                    mm = spread(dst[:, c, :], TILES + 1 + t, at)
                mm.then_inc(rot_ready, 1)

            pe.wait_ge(const_in, 32)
            for n, u in enumerate(PROLOGUE):
                if u == ("T", 0):
                    pe.wait_ge(split, 4)
                if n >= 2:
                    pe.wait_ge(unit_taken, n - 1 if n > 2 else 2)
                make(u, n)
            rotate(A, 0)
            pe.wait_ge(unit_taken, len(PROLOGUE))
            rotate(A, 1)
            pe.wait_ge(w0_ready, 1)
            pe.wait_ge(w_in, 16 * 10)

            def body(i, first, last, before_last):
                units = units_of(first, last)
                base = units_before(i, first)
                n = 0
                pool_n = 0
                for e in events(first, last):
                    if e[0] == "rot":
                        _, side, t, following = e
                        if following and t == 0:
                            pe.wait_ge(reduced, i * RED_PER_TILE + RED_X2[A])
                        elif following:
                            pe.wait_ge(unit_taken, base + len(units))
                        elif (side, t) == (Bs, 0):
                            if not first:
                                pe.wait_ge(reduced, i * RED_PER_TILE + (RED_X2[Bs] - RED_PER_TILE))
                        else:
                            pe.wait_ge(z_ready, z_after(i, 0, *((side, t - 2) if t >= 2 else (A, 3))))
                        rotate(side, t)
                    elif e[0] == "unit":
                        u = e[1]
                        if n >= 2:
                            pe.wait_ge(unit_taken, base + (n - 1))
                        if u == ("T", 0):
                            pe.wait_ge(split, i * 4 + 8)
                        if u == ("rep", 0, 0):
                            pe.wait_ge(unit_taken, base + (units.index(("T", 1)) + 1))
                        if u == ("h1", 0):
                            pe.wait_ge(reduced, i * RED_PER_TILE)
                            pe.wait_ge(ctx_in, i * 16)
                        if u[0] == "h2":
                            pe.wait_ge(unit_taken, base + (units.index(("h1", 1)) + 1))
                        if u[0] == "y":
                            pe.wait_ge(unit_taken, base + (units.index(("h2",)) + 1))
                        make(u, n)
                        n += 1
                    elif e[0] == "step":
                        _, layer, side, t = e
                        w = {0: w0_sb, 1: w1_sb, 2: w2_sb}[layer]
                        if layer == 0 and t == 0:
                            if not first:
                                pe.wait_ge(x3_ready, i * 2 + (side - 1))
                            for c in range(BLOCKS):
                                pe.matmul(acc[c * H:(c + 1) * H, side, :], w0d_sb[side * M:(side + 1) * M, :],
                                          squares[side * M:(side + 1) * M, c * COLS:(c + 1) * COLS],
                                          start=True, stop=False)
                        if layer and t in POOL_TILES:
                            src = z_pool[:, pool_n % POOL_SLOTS, :]
                            pool_n += 1
                            pe.wait_ge(z_pool_ready, i * POOL_Z_PER_TILE + pool_n)
                        else:
                            src = z[:, dve_steps().index((layer, side, t)) % SLOTS, :]
                            pe.wait_ge(z_ready, z_after(i, layer, side, t))
                        for c in range(BLOCKS):
                            mm = pe.matmul(acc[c * H:(c + 1) * H, side, :], w[:, t, :],
                                           src[:, c * COLS:(c + 1) * COLS],
                                           start=(layer > 0 and t == 0), stop=(t == STEPS[layer] - 1))
                        mm.then_inc(step_done, 1)

            over_tiles(pe, body)
            taken = units_before(NT - 1, False) + UNITS_LAST
            pe.wait_ge(reduced, NT * RED_PER_TILE)
            pe.wait_ge(ctx_in, NT * 16)
            for n, u in enumerate(EPILOGUE):
                pe.wait_ge(unit_taken, taken + (n if n >= 2 else 0))
                make(u, n)

        @block.scalar
        def _(act):
            def take(u, bank_n, ready, i):
                bank = stage[:, bank_n % 2, :]
                act.wait_ge(unit_ready, ready)
                if u[0] == "T":
                    src = bank.bitcast(BF16)[0:PARTS * M, :].rearrange("p (d q b) -> p d q b", q=SIDES * BLOCKS, b=ROWS)
                    dst = x0t[:, :].rearrange("p (q d b) -> p d q b", q=SIDES * BLOCKS, b=ROWS)
                    half = D // 2
                    op = act.activation(dst[:, u[1] * half:(u[1] + 1) * half], src, ACT.Copy)
                elif u[0] == "rep":
                    _, side, c = u
                    act.activation(x0four[:, side, c * COLS:(c + 1) * COLS], bank, ACT.Copy)
                    op = act.activation(squares[side * M:(side + 1) * M, c * COLS:(c + 1) * COLS],
                                        bank[side * M:(side + 1) * M, :], ACT.Square)
                elif u[0] in ("x0", "x0_next"):
                    _, side, t, c = u
                    op = act.activation(x0rep[:, side, t, c * COLS:(c + 1) * COLS], bank, ACT.Copy)
                elif u[0] == "h1":
                    for m in range(2 * u[1], 2 * u[1] + 2):
                        op = act.activation(h1[:, m, :], bank[:, (m % 2) * P:(m % 2 + 1) * P], ACT.Relu,
                                            bias=bt1_sb[:, m:m + 1])
                elif u[0] == "h2":
                    for m in range(F2 // P):
                        op = act.activation(h2[:, m, :], bank[:, m * P:(m + 1) * P], ACT.Relu,
                                            bias=bt2_sb[:, m:m + 1])
                else:
                    act.wait_ge(y_out, i * 16)
                    op = act.activation(y_sb[:], bank[0:1, 0:P], ACT.Copy)
                op.then_inc(unit_taken, 1)

            for n, u in enumerate(PROLOGUE):
                take(u, n, n + 1, None)

            def body(i, first, last, before_last):
                units = units_of(first, last)
                n = 0
                for e in events(first, last):
                    if e[0] == "unit":
                        if e[1] == ("h1", 0):
                            act.wait_ge(w_in, 16 * 10)
                        take(e[1], n, units_before(i, first) + (n + 1), i)
                        n += 1
                    elif e[0] == "end":
                        _, layer, side = e
                        act.wait_ge(step_done, i * STEPS_PER_TILE + (phase_start(layer, side) + STEPS[layer]))
                        if layer == 2:
                            if side == Bs:
                                act.wait_ge(reduced, i * RED_PER_TILE + RED_X3A)
                            elif not first:
                                act.wait_ge(reduced, i * RED_PER_TILE)
                            act.activation(x3[:], acc[:, side, :], ACT.Relu).then_inc(x3_ready, 1)
                            continue
                        if layer == 1:
                            act.wait_ge(reduced, i * RED_PER_TILE + RED_X1[side])
                        elif not first:
                            act.wait_ge(reduced, i * RED_PER_TILE + (RED_X2[side] - RED_PER_TILE))
                        for c in range(BLOCKS):
                            for half in range(2):
                                op = act.activation(xk[half * H:(half + 1) * H, side, c * COLS:(c + 1) * COLS],
                                                    acc[c * H:(c + 1) * H, side, :], ACT.Relu)
                        op.then_inc(xk_ready, 1)
                        ph = PHASES.index((layer, side)) + 1
                        act.wait_ge(xk_ready, i * 4 + ph)
                        act.activation(xk_copy[:, side, :], xk[:, side, :], ACT.Copy).then_inc(xk_copied, 1)

            over_tiles(act, body)
            for n, u in enumerate(EPILOGUE):
                take(u, n, units_before(NT - 1, False) + UNITS_LAST + n + 1, NT)

        @block.vector
        def _(dve):
            dve.wait_ge(w0_in, 32)
            dve.tensor_add(w0_sb[:, 0:TILES0 - 1, :], w0_sb[:, 0:TILES0 - 1, :], w0b_sb[:, 0:TILES0 - 1, :])
            dve.tensor_add(w0_sb[0:P - M, TILES0 - 1, :], w0_sb[0:P - M, TILES0 - 1, :],
                           w0b_sb[0:P - M, TILES0 - 1, :]).then_inc(w0_ready, 1)
            dve.wait_ge(w0_ready, 1)

            def sum_12(layer, side):
                lo = (layer - 1) * H
                src = xk[lo:lo + H, side, :].rearrange("p (c d b) -> p c b d", c=BLOCKS, d=D)
                dst = in12[lo:lo + H, side * BLOCKS * ROWS:(side + 1) * BLOCKS * ROWS].rearrange(
                    "p (c b) -> p c b", c=BLOCKS)
                dve.tensor_reduce(dst, src, AX_X, ALU.add).then_inc(reduced, 1)

            def sum_3(side, count):
                dve.wait_ge(x3_ready, count)
                for c in range(BLOCKS):
                    at = (side * BLOCKS + c) * ROWS
                    dve.tensor_reduce(in3[0:H, at:at + ROWS],
                                      x3[c * H:(c + 1) * H, :].rearrange("p (d b) -> p b d", d=D),
                                      AX_X, ALU.add).then_inc(reduced, 1)

            def body(i, first, last, before_last):
                units = units_of(first, last)
                for n, (layer, side, t) in enumerate(dve_steps()):
                    used = reuse_wait(dve_steps(), n, SLOTS, i)
                    if used is not None:
                        dve.wait_ge(step_done, used)
                    if layer == 0:
                        dve.wait_ge(rot_ready, i * ROTS_PER_TILE + (side * TILES0 + t + 1))
                        if (side, t) == (A, 0):
                            if first:
                                dve.wait_ge(unit_taken, len(PROLOGUE))
                            else:
                                dve.wait_ge(unit_taken, x0_units(i, first, A, 0))
                        src = stage if t % 2 else xk[:, side, :].rearrange("p (c n) -> p c n", c=BLOCKS)
                        dve.tensor_mul(z[:, n % SLOTS, :].rearrange("p (c n) -> p c n", c=BLOCKS), src[:, :, :],
                                       x0four[:, side, :].rearrange("p (c n) -> p c n", c=BLOCKS)
                                       ).then_inc(z_ready, 1)
                    else:
                        if layer == 1:
                            wait_x0(dve, i, first, side, t)
                        if t == 0:
                            dve.wait_ge(xk_copied, i * 4 + PHASES.index((layer, side)) - 1)
                        dve.tensor_mul(z[:, n % SLOTS, :], xk[:, side, :], x0rep[:, side, t, :]).then_inc(z_ready, 1)
                    if (layer, side, t) == (0, Bs, 1) and not first:
                        sum_3(Bs, i * 2)
                    if (layer, t) == (1, 10):
                        if side == A and not first:
                            dve.wait_ge(unit_ready, units_before(i, first) + (units.index(("h1", 1)) + 1))
                        sum_12(1, side)
                    if (layer, side, t) == (2, A, 6) or (layer, side, t) == (2, Bs, 8):
                        sum_12(2, side)
                    if (layer, side, t) == (2, Bs, 5):
                        sum_3(A, i * 2 + 1)

            over_tiles(dve, body)
            sum_3(Bs, 2 * NT)


def kernel(**inputs):
    import ml_dtypes
    import concourse.bacc as bacc
    from concourse.bass_utils import run_bass_kernel_spmd

    f = {k: np.asarray(v) for k, v in inputs.items()}
    row = np.arange(M)
    pick = np.zeros((M, TILES + 1 + TILES0, P), np.float32)
    for p in range(P):
        for t in range(TILES):
            pick[2 * t + p // H, t, p] = 1
        pick[p % M, TILES, p] = 1
        for t in range(TILES0):
            pick[(p + 4 * t + p // M + 1) % M, TILES + 1 + t, p] = 1
    sel = np.concatenate([pick] * PARTS).astype(ml_dtypes.bfloat16)
    s = 4 * np.arange(TILES0)[:, None, None] + np.arange(4)[None, :, None] + 1
    there = (row + s) % M
    here = np.broadcast_to(row, there.shape)
    w0 = f["L0_rec_W0"]
    as_w0 = lambda w: np.ascontiguousarray(w.reshape(TILES0, P, H).transpose(1, 0, 2))
    as_w = lambda w: np.ascontiguousarray(w.reshape(TILES, P, H).transpose(1, 0, 2))
    arrays = {
        "ids": f["ids"],
        "ctx_t": np.ascontiguousarray(f["dense_ctx"].T),
        **{f"tbl_{m}": f[f"tbl_{m}"] for m in range(M)},
        "sel": sel,
        "ident": np.eye(P, dtype=ml_dtypes.bfloat16),
        "w0a": as_w0(w0[here, there]),
        "w0b": as_w0(w0[there, here]),
        "w0d": np.ascontiguousarray(w0[row, row]),
        "w1": as_w(f["L0_rec_W1"]),
        "w2": as_w(f["L0_rec_W2"]),
        "wt1": f["W_top1"],
        "bt1": np.ascontiguousarray(f["b_top1"].reshape(F1 // P, P).T),
        "wt2": f["W_top2"],
        "bt2": np.ascontiguousarray(f["b_top2"].reshape(F2 // P, P).T),
        "wt3": np.ascontiguousarray(f["W_top3"].reshape(F2 // P, P).T),
    }
    nc = bacc.Bacc("TRN2", target_bir_lowering=False, num_devices=1)
    ap = {n: nc.dram_tensor(n, a.shape, mybir.dt.from_np(a.dtype), kind="ExternalInput").ap()
          for n, a in arrays.items()}
    out = nc.dram_tensor("y", (NT, P), F32, kind="ExternalOutput").ap()
    build(nc, ap["ids"], ap["ctx_t"], [ap[f"tbl_{m}"] for m in range(M)], ap["sel"], ap["ident"], ap["w0a"],
          ap["w0b"], ap["w0d"], ap["w1"], ap["w2"], ap["wt1"], ap["bt1"], ap["wt2"], ap["bt2"], ap["wt3"], out)
    r = run_bass_kernel_spmd(nc, [arrays], core_ids=[0])
    return r.results[0]["y"].reshape(B, 1)
```

```python
from contextlib import ExitStack

import numpy as np

import concourse.bass as bass
from concourse import mybir

F32 = mybir.dt.float32
BF16 = mybir.dt.bfloat16
I32 = mybir.dt.int32
ALU = mybir.AluOpType
ACT = mybir.ActivationFunctionType
AX_X = mybir.AxisListType.X

B, M, D = 1024, 32, 16
H = 64
P = 128
NT = B // P
SIDES, BLOCKS, ROWS = 2, 2, 32
COLS = D * ROWS
WIDE = BLOCKS * COLS
TILES = M * H // P
TILES0 = 16 * M // P
F1, F2 = 512, 256
NCTX = 16
PARTS = 3
K3 = H + NCTX
A, Bs = 0, 1

POOL_TILES = {(layer, side): (4, 9, 14) for layer in (1, 2) for side in (A, Bs)}
V, W, X = range(3)
ROTATIONS = np.array([[1, 2, 3, 4], [6, 9, 11, 14], [12, 13, 15, 16]])
ROTS_PER_TILE = SIDES * len(ROTATIONS)
UV, UW, VW, UX = range(TILES0)

DMA_TILES = (1, 2, 3, 5, 6, 7, 9, 10, 11, 12, 13, 14, 15)
PE_TILES = [t for t in range(TILES) if t not in DMA_TILES]
X0_AHEAD = len(PE_TILES) - 1
COPIES = P // M
PITCH = 2 * WIDE + 64
SLOTS, POOL_SLOTS = 3, 2
EARLY = 16
BETWEEN = {True: (4, 4, 4, 4), False: (13, 2, 1)}
SPLIT_AFTER = {True: 6, False: 3}
WARM_UP, KEEP_WARM = 28, 3
SPLIT_GROUPS = (range(0, 12), range(12, 22), range(22, 29), range(29, 32))

PHASES = [(0, A), (0, Bs), (1, A), (1, Bs), (2, A), (2, Bs)]
STEPS = {0: TILES0, 1: TILES, 2: TILES}


def phase_start(layer, side):
    return sum(STEPS[l] for l, s in PHASES[: PHASES.index((layer, side))])


STEPS_PER_TILE = sum(STEPS[l] for l, _ in PHASES)
POOL_Z_PER_TILE = sum(len(tiles) for tiles in POOL_TILES.values())
DVE_Z_PER_TILE = STEPS_PER_TILE - POOL_Z_PER_TILE



def pairs(kind, side):
    return [(kind, side, t, c) for t in PE_TILES for c in range(BLOCKS)]


def make_units(first, last):
    at = {}

    def put(units, layer, side, step, per_step, quiet=3):
        steps = [(l, s, t) for l, s in PHASES for t in range(STEPS[l]) if t >= quiet]
        start = steps.index((layer, side, step))
        for n, u in enumerate(units):
            at.setdefault(steps[start + int(n / per_step)], []).append(u)

    if first:
        put(pairs("x0", A)[:4], 0, Bs, TILES0 - 1, 4, quiet=0)
        put(pairs("x0", A)[4:] + pairs("x0", Bs), 1, A, 0, 1.2, quiet=0)
    else:
        ahead = BLOCKS * X0_AHEAD
        put([("h1", 0), ("h1", 1)], 0, Bs, TILES0 - 1, 2, quiet=0)
        put(pairs("x0", Bs)[:ahead], 1, A, 7, 0.7)
        put(pairs("x0", Bs)[ahead:], 1, Bs, 3, 1)
    if not first:
        put([("h2",)], 2, A, 3, 1)
        put([("y",)], 2, A, 7, 1)
    if not last and not first:
        put(pairs("x0_next", A), 2, A, 9, 0.4)
    if not last:
        prepare = [("T", 0), ("T", 1)] + [("rep", s, c) for s in range(SIDES) for c in range(BLOCKS)]
        if first:
            put(prepare, 2, A, 3, 1.5)
            put(pairs("x0_next", A), 2, A, 9, 0.4)
        else:
            put(prepare, 1, Bs, 8, 1)
    return at


def events(first, last):
    at = make_units(first, last)
    out = []
    rots = {(A, 1): (A, X), (A, 2): (Bs, V), (A, 3): (Bs, W), (Bs, 1): (Bs, X)}
    for layer, side in PHASES:
        for step in range(STEPS[layer]):
            if layer == 0 and (side, step) in rots:
                out.append(("rot", *rots[side, step], False))
            out.append(("step", layer, side, step))
            out += [("unit", u) for u in at.get((layer, side, step), [])]
            if (layer, side, step) == (2, Bs, TILES - 2) and not last:
                out += [("rot", A, V, True), ("rot", A, W, True)]
        out.append(("end", layer, side))
    return out


def units_of(first, last):
    return [e[1] for e in events(first, last) if e[0] == "unit"]


PROLOGUE = [("T", 0), ("T", 1)] + [("rep", s, c) for s in range(SIDES) for c in range(BLOCKS)]
REPS_FIRST = {A: 4, Bs: 6}
EPILOGUE = [("h1", 0), ("h1", 1), ("h2",), ("y",)]
UNITS_FIRST, UNITS_TILE, UNITS_LAST = (len(units_of(*x)) for x in ((True, False), (False, False), (False, True)))
assert not (len(PROLOGUE) % 2 or UNITS_FIRST % 2 or UNITS_TILE % 2 or UNITS_LAST % 2)
assert units_of(True, False)[-BLOCKS * len(PE_TILES):] == units_of(False, False)[-BLOCKS * len(PE_TILES):] == pairs("x0_next", A)


def units_before(i, first):
    return len(PROLOGUE) if first else i * UNITS_TILE + (len(PROLOGUE) + UNITS_FIRST - UNITS_TILE)


def x0_units(i, first, side, t):
    if first or side == Bs:
        return units_before(i, first) + (units_of(first, False).index(("x0", side, t, BLOCKS - 1)) + 1)
    return units_before(i, first) + (BLOCKS * (PE_TILES.index(t) + 1) - BLOCKS * len(PE_TILES))


def dve_steps():
    return [(l, s, t) for l, s in PHASES for t in range(STEPS[l]) if t not in POOL_TILES.get((l, s), ())]


def pool_steps():
    return [(l, s, t) for l, s in PHASES for t in POOL_TILES.get((l, s), ())]


def z_after(i, layer, side, t):
    return i * DVE_Z_PER_TILE + (dve_steps().index((layer, side, t)) + 1)


def slots_of(count, slots):
    turn = [n % slots for n in range(count)]
    if turn[-1] == 0:
        turn[-1] = 1
    return turn


def reuse_wait(steps, n, turn, i):
    back = next(b for b in range(1, len(steps)) if turn[n - b] == turn[n])
    l, s, t = steps[n - back]
    done = phase_start(l, s) + t + 1
    if n >= back:
        return i * STEPS_PER_TILE + done
    if isinstance(i, int) and i == 0:
        return None
    return i * STEPS_PER_TILE + (done - STEPS_PER_TILE)


DVE_TURN = slots_of(DVE_Z_PER_TILE, SLOTS)
POOL_TURN = slots_of(POOL_Z_PER_TILE, POOL_SLOTS)
V_SLOT_OF = POOL_Z_PER_TILE - 2
assert POOL_TURN[V_SLOT_OF] == POOL_TURN[0] != POOL_TURN[-1]


SUM_AT = {(0, A, 2): (2, Bs), (1, A, 1): (0, A), (1, A, 7): (0, Bs), (1, Bs, 6): (1, A), (2, A, 6): (1, Bs),
          (2, Bs, 6): (2, A)}
INPUTS_AT = {(0, A): [(2, Bs)], (1, A): [(0, A), (0, Bs)], (1, Bs): [(1, A)], (2, A): [(1, Bs)], (2, Bs): [(2, A)]}


def outputs_before(i, layer, side):
    return i * len(PHASES) + PHASES.index((layer, side))


def build(nc, ids, ctx_t, tables, sel, ident, w0a, w0b, w0d, w1, w2, wt1, bt1, wt2, bt2, wt3, out):
    with ExitStack() as stack:
        def sb(name, shape, dt=F32):
            return stack.enter_context(nc.sbuf_tensor(name, shape, dt))

        def sem(name):
            return stack.enter_context(nc.semaphore(name))

        sel_sb = sb("sel_sb", [PARTS * M, TILES + 1 + len(ROTATIONS), P], BF16)
        ident_sb = sb("ident_sb", [P, P], BF16)
        w0_sb = sb("w0_sb", [P, TILES0, H])
        w0d_sb = sb("w0d_sb", [2 * M, H])
        w1_sb = sb("w1_sb", [P, TILES, H])
        w2_sb = sb("w2_sb", [P, TILES, H])
        wt1_sb = sb("wt1_sb", [P, 2, F1])
        wt2_sb = sb("wt2_sb", [P, F1 // P, F2])
        wt3_sb = sb("wt3_sb", [P, F2 // P])
        bt1_sb = sb("bt1_sb", [P, F1 // P])
        bt2_sb = sb("bt2_sb", [P, F2 // P])
        ones = sb("ones", [P, 1])
        idx = sb("idx", [P, M], I32)
        emb = sb("emb", [P, M, D])
        parts = sb("parts", [P, D, PARTS, M], BF16)
        x0t = sb("x0t", [PARTS * M, SIDES * WIDE], BF16)
        x0rep = sb("x0rep", [P, SIDES, TILES, WIDE])
        x0four = sb("x0four", [P, SIDES, WIDE])
        squares = sb("squares", [SIDES * M, WIDE])
        xk_copy = sb("xk_copy", [P, SIDES, WIDE])
        z = sb("z", [P, SLOTS, WIDE])
        z_pool = sb("z_pool", [P, POOL_SLOTS, WIDE])
        layer_out = sb("layer_out", [P, COLS])
        row_sums = sb("row_sums", [P, len(PHASES), ROWS])
        in12 = sb("in12", [P, P])
        in3 = sb("in3", [K3, P])
        h1 = sb("h1", [P, F1 // P, P])
        h2 = sb("h2", [P, F2 // P, P])
        y_sb = sb("y_sb", [1, P])
        w0b_sb = z[:, 0, 0:TILES0 * H].rearrange("p (t k) -> p t k", t=TILES0)

        v_copy = z_pool[:, POOL_TURN[V_SLOT_OF], :]

        xk = stack.enter_context(nc.psum_tensor("xk", [P, SIDES, WIDE], F32))
        acc = stack.enter_context(nc.psum_tensor("acc", [P, SIDES, COLS], F32))
        stage = stack.enter_context(nc.psum_tensor("stage", [P, 2, COLS], F32))

        const_in = sem("const_in")
        w0_in = sem("w0_in")
        w_in = sem("w_in")
        idx_in = sem("idx_in")
        ctx_in = sem("ctx_in")
        gathered = sem("gathered")
        ones_set = sem("ones_set")
        x0_saved = [sem(f"x0_saved{side}") for side in range(SIDES)]
        x0_loaded = [{t: sem(f"x0_loaded{side}_{t}") for t in DMA_TILES} for side in range(SIDES)]
        gathered_first = [sem(f"gathered_first{g}") for g in range(len(SPLIT_GROUPS))]
        split_first = sem("split_first")
        squares_first = sem("squares_first")
        split = sem("split")
        w0_ready = sem("w0_ready")
        unit_ready = sem("unit_ready")
        unit_taken = sem("unit_taken")
        rot_ready = sem("rot_ready")
        v_copied = sem("v_copied")
        z_ready = sem("z_ready")
        z_pool_ready = sem("z_pool_ready")
        step_done = sem("step_done")
        xk_ready = sem("xk_ready")
        xk_copied = sem("xk_copied")
        layer_out_ready = sem("layer_out_ready")
        reduced = sem("reduced")
        inputs_in = sem("inputs_in")
        y_out = sem("y_out")

        x0_dram = nc.dram_tensor("x0_dram", (SIDES, COPIES, M, PITCH), F32).ap()

        block = stack.enter_context(nc.Block())

        def wait_x0(eng, i, first, side, t):
            if t in DMA_TILES:
                eng.wait_ge(x0_loaded[side][t], i * 32 + 32)
            else:
                eng.wait_ge(unit_taken, x0_units(i, first, side, t))

        def split_operations(group):
            lo, hi = group[0], group[-1] + 1
            whole = emb[:, lo:hi, :]
            one = ones[:, 0:1].unsqueeze(2).to_broadcast([P, hi - lo, D])
            part = [parts[:, :, n, lo:hi].rearrange("p d m -> p m d") for n in range(PARTS)]
            return [("mul", part[0], whole, one), ("sub", whole, whole, part[0]),
                    ("mul", part[1], whole, one), ("sub", part[2], whole, part[1])]

        def prologue_bank(n):
            return [stage[:, 0, :], stage[:, 1, :], stage[:, 0, :], stage[:, 1, :], acc[:, Bs, :],
                    xk[:, Bs, 0:COLS]][n]

        def over_tiles(eng, body, tail=1):
            body(0, True, False, False)
            with eng.Fori(1, NT - tail) as i:
                body(i, False, False, False)
            for i in range(NT - tail, NT):
                body(i, False, i == NT - 1, i == NT - 2)

        @block.sync
        def _(sp):
            sp.sem_inc(y_out, 16)
            sp.dma_start(idx[:], ids[0:P, :]).then_inc(idx_in, 16)
            sp.dma_start(sel_sb[:], sel).then_inc(const_in, 16)
            sp.dma_start(ident_sb[:], ident).then_inc(const_in, 16)
            sp.dma_start(w0_sb[:], w0a).then_inc(w0_in, 16)
            sp.dma_start(w0b_sb, w0b).then_inc(w0_in, 16)
            for s in range(SIDES):
                sp.dma_start(w0d_sb[s * M:(s + 1) * M, :], w0d).then_inc(w_in, 16)
            sp.dma_start(w1_sb[:], w1).then_inc(w_in, 16)
            sp.dma_start(w2_sb[:], w2).then_inc(w_in, 16)
            sp.dma_start(wt1_sb[:, 0, :], wt1[0:P, :]).then_inc(w_in, 16)
            sp.dma_start(wt1_sb[0:K3, 1, :], wt1[P:P + K3, :]).then_inc(w_in, 16)
            sp.dma_start(wt2_sb[:], wt2.rearrange("(t p) n -> p t n", p=P)).then_inc(w_in, 16)
            sp.dma_start(wt3_sb[:], wt3).then_inc(w_in, 16)
            sp.dma_start(bt1_sb[:], bt1).then_inc(w_in, 16)
            sp.dma_start(bt2_sb[:], bt2).then_inc(w_in, 16)
            for g, group in enumerate(SPLIT_GROUPS):
                sp.wait_ge(gathered_first[g], 16 * len(group))
            sp.dma_start(idx[:], ids[P:2 * P, :]).then_inc(idx_in, 16)

            def save_x0(side):
                sp.dma_start(x0_dram[side, :, :, 0:WIDE].rearrange("r m n -> (r m) n"),
                             x0four[:, side, :]).then_inc(x0_saved[side], 16)

            def load_x0(side, t):
                for j in range(P // H):
                    sp.dma_start(x0rep[j * H:(j + 1) * H, side, t, :],
                                 x0_dram[side, :, 2 * t + j, 0:WIDE].unsqueeze(1).to_broadcast(
                                     [COPIES, H // COPIES, WIDE])).then_inc(x0_loaded[side][t], 16)

            for side in range(SIDES):
                sp.wait_ge(unit_taken, REPS_FIRST[side])
                save_x0(side)
            for side in range(SIDES):
                sp.wait_ge(x0_saved[side], 16)
                for t in DMA_TILES:
                    load_x0(side, t)

            def body(i, first, last, before_last):
                units = units_of(first, last)
                if not first:
                    sp.wait_ge(unit_ready, units_before(i, first) + (units.index(("h1", 1)) + 1))
                sp.dma_start(in3[H:K3, :], ctx_t[:, bass.ds(i * P, P)]).then_inc(ctx_in, 16)
                if not last and not before_last:
                    sp.wait_ge(gathered, i * (16 * M) + 16 * M)
                    sp.dma_start(idx[:], ids[bass.ds(i * P + 2 * P, P), :]).then_inc(idx_in, 16)

                if not last:
                    def value(v):
                        return v if isinstance(i, int) else sp.to_reg(v)

                    for side in range(SIDES):
                        used = value(i * STEPS_PER_TILE + (phase_start(1, side) + TILES))
                        filled = value(units_before(i, first) + (units.index(("rep", side, 1)) + 1))
                        sp.wait_ge(step_done, used)
                        sp.wait_ge(unit_taken, filled)
                        save_x0(side)
                    def loads(side):
                        for n, t in enumerate(DMA_TILES):
                            saved = value(i * 16 + 32)
                            used = value(i * STEPS_PER_TILE + (phase_start(2, side) + t + 1))
                            if n == 0:
                                sp.wait_ge(x0_saved[side], saved)
                            sp.wait_ge(step_done, used)
                            load_x0(side, t)

                    loads(A)
                if not first:
                    sp.wait_ge(unit_taken, units_before(i, first) + (units.index(("y",)) + 1))
                    sp.dma_start(out[bass.ds(i - 1, 1), :], y_sb[:]).then_inc(y_out, 16)
                if not last:
                    loads(Bs)

            over_tiles(sp, body, tail=2)
            sp.wait_ge(unit_taken, units_before(NT - 1, False) + UNITS_LAST + len(EPILOGUE))
            sp.dma_start(out[NT - 1:NT, :], y_sb[:]).then_inc(y_out, 16)
            sp.wait_ge(y_out, 16 * NT + 16)

        @block.gpsimd
        def _(pool):
            def gathers(tables_now, landed=gathered):
                for m in tables_now:
                    pool.indirect_dma_start(
                        out=emb[:, m, :], out_offset=None, in_=tables[m],
                        in_offset=bass.IndirectOffsetOnAxis(ap=idx[:, m:m + 1], axis=0),
                    ).then_inc(landed, 16)

            def split_parts(j):
                pool.wait_ge(gathered, j * (16 * M))
                operations = split_operations(range(M))
                for n, (op, *args) in enumerate(operations):
                    if n:
                        pool.wait_ge(split, j * len(operations) + (n - len(operations)))
                    pool_op = pool.tensor_mul if op == "mul" else pool.tensor_sub
                    pool_op(*args).then_inc(split, 1)

            pool.memset(ones[:], 1.0).then_inc(ones_set, 1)
            pool.wait_ge(idx_in, 16)
            for g, group in enumerate(SPLIT_GROUPS):
                gathers(group, gathered_first[g])
            pool.wait_ge(split_first, 4 * len(SPLIT_GROUPS))
            pool.wait_ge(ones_set, 1)
            pool.wait_ge(idx_in, 32)
            gathers(range(EARLY))

            def body(i, first, last, before_last):
                units = units_of(first, last)
                steps = pool_steps()

                def product(n):
                    layer, side, t = steps[n]
                    if layer == 1:
                        wait_x0(pool, i, first, side, t)
                    if n == 0:
                        pool.wait_ge(z_ready, z_after(i, 0, Bs, VW))
                    pool.wait_ge(xk_copied, i * 4 + PHASES.index((layer, side)) - 1)
                    used = reuse_wait(steps, n, POOL_TURN, i)
                    if used is not None:
                        pool.wait_ge(step_done, used)
                    pool.tensor_mul(z_pool[:, POOL_TURN[n], :], x0rep[:, side, t, :],
                                    xk_copy[:, side, :]).then_inc(z_pool_ready, 1)

                now, done = EARLY, 0
                for n in range(POOL_Z_PER_TILE):
                    if n < len(BETWEEN[first]) and not last:
                        gathers(range(now, now + BETWEEN[first][n]))
                        now += BETWEEN[first][n]
                    if n == SPLIT_AFTER[first] and not last:
                        pool.wait_ge(unit_ready, units_before(i, first))
                        split_parts(i + 1)
                        if not before_last:
                            pool.wait_ge(split, i * 4 + 4)
                            pool.wait_ge(idx_in, i * 16 + 48)
                    product(n)
                    if n >= SPLIT_AFTER[first] and not last and not before_last:
                        more = EARLY * (n - SPLIT_AFTER[first] + 1) // (POOL_Z_PER_TILE - SPLIT_AFTER[first])
                        gathers(range(done, more))
                        done = more

            over_tiles(pool, body, tail=2)

        @block.tensor
        def _(pe):
            def spread(dst, w, at):
                for h in range(2):
                    mm = pe.matmul(dst[h * H:(h + 1) * H, :], sel_sb[:, w, h * H:(h + 1) * H],
                                   x0t[:, at:at + COLS], start=True, stop=True)
                return mm

            def make(u, n, bank=None):
                bank = stage[:, n % 2, :] if bank is None else bank
                if u[0] == "T":
                    bank = bank.bitcast(BF16)
                    for k in range(D // 2):
                        d = u[1] * (D // 2) + k
                        last = pe.transpose(bank[0:PARTS * M, k * P:(k + 1) * P],
                                            parts[:, d, :, :].rearrange("p a m -> p (a m)"), ident_sb[:])
                elif u[0] in ("rep", "x0", "x0_next"):
                    w = TILES if u[0] == "rep" else u[2]
                    side, c = u[1], u[-1]
                    at = (side * BLOCKS + c) * COLS
                    last = spread(bank, w, at)
                elif u[0] == "h1":
                    for m in range(2 * u[1], 2 * u[1] + 2):
                        o = bank[:, (m % 2) * P:(m % 2 + 1) * P]
                        pe.matmul(o, wt1_sb[:, 0, m * P:(m + 1) * P], in12[:], start=True, stop=False)
                        last = pe.matmul(o, wt1_sb[0:K3, 1, m * P:(m + 1) * P], in3[:], start=False, stop=True)
                elif u[0] == "h2":
                    for m in range(F2 // P):
                        for k in range(F1 // P):
                            last = pe.matmul(bank[:, m * P:(m + 1) * P], wt2_sb[:, k, m * P:(m + 1) * P],
                                             h1[:, k, :], start=(k == 0), stop=(k == F1 // P - 1))
                else:
                    for k in range(F2 // P):
                        last = pe.matmul(bank[0:1, 0:P], wt3_sb[:, k:k + 1], h2[:, k, :],
                                         start=(k == 0), stop=(k == F2 // P - 1))
                last.then_inc(unit_ready, 1)

            def rotate(side, t):
                dst = stage if t == W else xk[:, side, :].rearrange("p (c n) -> p c n", c=BLOCKS)
                for c in range(BLOCKS):
                    at = (side * BLOCKS + c) * COLS
                    mm = spread(dst[:, c, :], TILES + 1 + t, at)
                mm.then_inc(rot_ready, 1)

            pe.wait_ge(const_in, 32)
            def keep_busy(count):
                for n in range(count):
                    pe.matmul(acc[:, 0, :], sel_sb[:, TILES, :],
                              sel_sb[:, 0:COLS // P, :].rearrange("p t n -> p (t n)"), start=True, stop=True)

            pe.wait_ge(gathered_first[-3], 16 * len(SPLIT_GROUPS[-3]))
            keep_busy(WARM_UP)
            for n, u in enumerate(PROLOGUE):
                if u == ("T", 0):
                    pe.wait_ge(split_first, 4 * len(SPLIT_GROUPS))
                if n == 2:
                    pe.wait_ge(unit_taken, 2)
                make(u, n, prologue_bank(n))
                if n == 1:
                    keep_busy(KEEP_WARM)
                if n + 1 == REPS_FIRST[A]:
                    rotate(A, V)
            keep_busy(KEEP_WARM)
            pe.wait_ge(unit_taken, REPS_FIRST[A])
            rotate(A, W)
            keep_busy(KEEP_WARM)
            pe.wait_ge(w0_ready, 1)
            pe.wait_ge(w_in, 16 * 10)

            def body(i, first, last, before_last):
                units = units_of(first, last)
                base = units_before(i, first)
                n = 0
                pool_n = 0
                for e in events(first, last):
                    if e[0] == "rot":
                        _, side, t, following = e
                        if first and (side, t) == (Bs, V):
                            pe.wait_ge(unit_taken, REPS_FIRST[Bs])
                        if t == X:
                            pe.wait_ge(z_ready, z_after(i, 0, side, UV))
                        elif t == W and following:
                            pe.wait_ge(unit_taken, base + len(units))
                        elif t == W:
                            pe.wait_ge(z_ready, z_after(i, 0, A, VW))
                        rotate(side, t)
                    elif e[0] == "unit":
                        u = e[1]
                        if n >= 2:
                            pe.wait_ge(unit_taken, base + (n - 1))
                        if u == ("T", 0):
                            pe.wait_ge(split, i * 4 + 4)
                        if u == ("rep", 0, 0):
                            pe.wait_ge(unit_taken, base + (units.index(("T", 1)) + 1))
                        if u == ("h1", 0):
                            pe.wait_ge(inputs_in, i * len(INPUTS_AT))
                            pe.wait_ge(ctx_in, i * 16)
                        if u[0] == "h2":
                            pe.wait_ge(unit_taken, base + (units.index(("h1", 1)) + 1))
                        if u[0] == "y":
                            pe.wait_ge(unit_taken, base + (units.index(("h2",)) + 1))
                        make(u, n)
                        n += 1
                    elif e[0] == "step":
                        _, layer, side, t = e
                        w = {0: w0_sb, 1: w1_sb, 2: w2_sb}[layer]
                        if t == 0 and not (first and layer == 0):
                            pe.wait_ge(layer_out_ready, outputs_before(i, (layer + 2) % 3, side) +
                                       (1 if layer else 1 - len(PHASES)))
                        if first and layer == 0 and t == 0:
                            if side == A:
                                pe.wait_ge(squares_first, 1)
                            else:
                                pe.wait_ge(unit_taken, REPS_FIRST[Bs])
                        if layer == 0 and t == 0:
                            for c in range(BLOCKS):
                                pe.matmul(acc[c * H:(c + 1) * H, side, :], w0d_sb[side * M:(side + 1) * M, :],
                                          squares[side * M:(side + 1) * M, c * COLS:(c + 1) * COLS],
                                          start=True, stop=False)
                        if t in POOL_TILES.get((layer, side), ()):
                            src = z_pool[:, POOL_TURN[pool_n], :]
                            pool_n += 1
                            pe.wait_ge(z_pool_ready, i * POOL_Z_PER_TILE + pool_n)
                        else:
                            src = z[:, DVE_TURN[dve_steps().index((layer, side, t))], :]
                            pe.wait_ge(z_ready, z_after(i, layer, side, t))
                        for c in range(BLOCKS):
                            mm = pe.matmul(acc[c * H:(c + 1) * H, side, :], w[:, t, :],
                                           src[:, c * COLS:(c + 1) * COLS],
                                           start=(layer > 0 and t == 0), stop=(t == STEPS[layer] - 1))
                        mm.then_inc(step_done, 1)

            over_tiles(pe, body)
            taken = units_before(NT - 1, False) + UNITS_LAST
            pe.wait_ge(inputs_in, NT * len(INPUTS_AT))
            pe.wait_ge(ctx_in, NT * 16)
            for n, u in enumerate(EPILOGUE):
                pe.wait_ge(unit_taken, taken + (n if n >= 2 else 0))
                make(u, n)

        @block.scalar
        def _(act):
            def take(u, bank_n, ready, i, bank=None, square=True):
                bank = stage[:, bank_n % 2, :] if bank is None else bank
                act.wait_ge(unit_ready, ready)
                if u[0] == "T":
                    src = bank.bitcast(BF16)[0:PARTS * M, :].rearrange("p (d q b) -> p d q b", q=SIDES * BLOCKS, b=ROWS)
                    dst = x0t[:, :].rearrange("p (q d b) -> p d q b", q=SIDES * BLOCKS, b=ROWS)
                    half = D // 2
                    op = act.activation(dst[:, u[1] * half:(u[1] + 1) * half], src, ACT.Copy)
                elif u[0] == "rep":
                    _, side, c = u
                    op = act.activation(x0four[:, side, c * COLS:(c + 1) * COLS], bank, ACT.Copy)
                    if square:
                        op = act.activation(squares[side * M:(side + 1) * M, c * COLS:(c + 1) * COLS],
                                            bank[side * M:(side + 1) * M, :], ACT.Square)
                elif u[0] in ("x0", "x0_next"):
                    _, side, t, c = u
                    op = act.activation(x0rep[:, side, t, c * COLS:(c + 1) * COLS], bank, ACT.Copy)
                elif u[0] == "h1":
                    for m in range(2 * u[1], 2 * u[1] + 2):
                        op = act.activation(h1[:, m, :], bank[:, (m % 2) * P:(m % 2 + 1) * P], ACT.Relu,
                                            bias=bt1_sb[:, m:m + 1])
                elif u[0] == "h2":
                    for m in range(F2 // P):
                        op = act.activation(h2[:, m, :], bank[:, m * P:(m + 1) * P], ACT.Relu,
                                            bias=bt2_sb[:, m:m + 1])
                else:
                    act.wait_ge(y_out, i * 16)
                    op = act.activation(y_sb[:], bank[0:1, 0:P], ACT.Copy)
                op.then_inc(unit_taken, 1)

            def inputs(phases):
                for layer, side in phases:
                    dst = in12[layer * H:(layer + 1) * H, :] if layer < 2 else in3[0:H, :]
                    for c in range(BLOCKS):
                        at = (side * BLOCKS + c) * ROWS
                        op = act.activation(dst[:, at:at + ROWS],
                                            row_sums[c * H:(c + 1) * H, PHASES.index((layer, side)), :], ACT.Copy)
                op.then_inc(inputs_in, 1)

            def copy_v(side, rots):
                act.wait_ge(rot_ready, rots)
                act.activation(v_copy, xk[:, side, :], ACT.Copy).then_inc(v_copied, 1)

            for n, u in enumerate(PROLOGUE):
                take(u, n, n + 1, None, prologue_bank(n), square=(n >= REPS_FIRST[A]))
                if n + 1 == REPS_FIRST[A]:
                    act.wait_ge(unit_taken, REPS_FIRST[A])
                    act.activation(squares[0:M, :], x0four[0:M, A, :], ACT.Square).then_inc(squares_first, 1)
                    copy_v(A, 1)

            def body(i, first, last, before_last):
                units = units_of(first, last)
                n = 0
                for e in events(first, last):
                    if e[0] == "unit":
                        if e[1] == ("h1", 0):
                            act.wait_ge(w_in, 16 * 10)
                        take(e[1], n, units_before(i, first) + (n + 1), i)
                        n += 1
                    elif e[0] == "rot" and e[2] == V:
                        if e[1] == A:
                            _, side, t = pool_steps()[V_SLOT_OF]
                            act.wait_ge(step_done, i * STEPS_PER_TILE + (phase_start(2, side) + t + 1))
                            copy_v(A, i * ROTS_PER_TILE + (ROTS_PER_TILE + 1))
                        else:
                            act.wait_ge(z_ready, z_after(i, 0, A, VW))
                            copy_v(Bs, i * ROTS_PER_TILE + (len(ROTATIONS) + 1))
                    elif e[0] == "end":
                        _, layer, side = e
                        act.wait_ge(step_done, i * STEPS_PER_TILE + (phase_start(layer, side) + STEPS[layer]))
                        if layer < 2:
                            for into, landed in ((xk, xk_ready), (xk_copy, xk_copied)):
                                for c in range(BLOCKS):
                                    for half in range(2):
                                        op = act.activation(
                                            into[half * H:(half + 1) * H, side, c * COLS:(c + 1) * COLS],
                                            acc[c * H:(c + 1) * H, side, :], ACT.Relu)
                                op.then_inc(landed, 1)
                        before = outputs_before(i, layer, side)
                        if not (first and (layer, side) == (0, A)):
                            act.wait_ge(reduced, before)
                        act.activation(layer_out[:], acc[:, side, :], ACT.Relu).then_inc(layer_out_ready, 1)
                        if (layer, side) in INPUTS_AT and not (first and (layer, side) == (0, A)):
                            inputs(INPUTS_AT[layer, side])

            over_tiles(act, body)
            act.wait_ge(reduced, NT * len(PHASES))
            inputs(INPUTS_AT[0, A])
            for n, u in enumerate(EPILOGUE):
                take(u, n, units_before(NT - 1, False) + UNITS_LAST + n + 1, NT)

        @block.vector
        def _(dve):
            dve.wait_ge(w0_in, 32)
            dve.tensor_add(w0_sb[:, 0:TILES0 - 1, :], w0_sb[:, 0:TILES0 - 1, :], w0b_sb[:, 0:TILES0 - 1, :])
            dve.tensor_add(w0_sb[0:P - M, TILES0 - 1, :], w0_sb[0:P - M, TILES0 - 1, :],
                           w0b_sb[0:P - M, TILES0 - 1, :]).then_inc(w0_ready, 1)
            dve.wait_ge(w0_ready, 1)
            dve.wait_ge(ones_set, 1)
            n = 0
            for g, group in enumerate(SPLIT_GROUPS):
                dve.wait_ge(gathered_first[g], 16 * len(group))
                for k, (op, *args) in enumerate(split_operations(group)):
                    if k:
                        dve.wait_ge(split_first, n)
                    dve_op = dve.tensor_mul if op == "mul" else dve.tensor_sub
                    dve_op(*args).then_inc(split_first, 1)
                    n += 1

            def sum_over_d(phase, ready):
                dve.wait_ge(layer_out_ready, ready)
                dve.tensor_reduce(row_sums[:, PHASES.index(phase), :],
                                  layer_out[:].rearrange("p (d b) -> p b d", d=D), AX_X, ALU.add
                                  ).then_inc(reduced, 1)

            def body(i, first, last, before_last):
                for n, (layer, side, t) in enumerate(dve_steps()):
                    used = reuse_wait(dve_steps(), n, DVE_TURN, i)
                    if used is not None:
                        dve.wait_ge(step_done, used)
                    if layer == 0:
                        rot = {UV: V, UW: W, VW: W, UX: X}[t]
                        dve.wait_ge(rot_ready, i * ROTS_PER_TILE + (side * len(ROTATIONS) + rot + 1))
                        if (side, t) == (A, UV):
                            if first:
                                dve.wait_ge(unit_taken, REPS_FIRST[A])
                            else:
                                dve.wait_ge(unit_taken, x0_units(i, first, A, 0))
                        if first and (side, t) == (Bs, UV):
                            dve.wait_ge(unit_taken, REPS_FIRST[Bs])
                        if t == UV:
                            dve.wait_ge(v_copied, i * SIDES + (side + 1))
                        src = stage if rot == W else xk[:, side, :].rearrange("p (c n) -> p c n", c=BLOCKS)
                        other = v_copy if t == VW else x0four[:, side, :]
                        dve.tensor_mul(z[:, DVE_TURN[n], :].rearrange("p (c n) -> p c n", c=BLOCKS), src[:, :, :],
                                       other.rearrange("p (c n) -> p c n", c=BLOCKS)).then_inc(z_ready, 1)
                    else:
                        if layer == 1:
                            wait_x0(dve, i, first, side, t)
                        if t == 0:
                            dve.wait_ge(xk_ready, i * 4 + PHASES.index((layer, side)) - 1)
                        dve.tensor_mul(z[:, DVE_TURN[n], :], xk[:, side, :], x0rep[:, side, t, :]).then_inc(z_ready, 1)
                    if (layer, side, t) in SUM_AT:
                        phase = SUM_AT[layer, side, t]
                        if phase != (2, Bs):
                            sum_over_d(phase, outputs_before(i, *phase) + 1)
                        elif not first:
                            sum_over_d(phase, i * len(PHASES))

            over_tiles(dve, body)
            sum_over_d((2, Bs), NT * len(PHASES))


def kernel(**inputs):
    import ml_dtypes
    import concourse.bacc as bacc
    from concourse.bass_utils import run_bass_kernel_spmd

    f = {k: np.asarray(v) for k, v in inputs.items()}
    row = np.arange(M)
    pick = np.zeros((M, TILES + 1 + len(ROTATIONS), P), np.float32)
    for p in range(P):
        for t in range(TILES):
            pick[2 * t + p // H, t, p] = 1
        pick[p % M, TILES, p] = 1
        for r in range(len(ROTATIONS)):
            pick[(p + ROTATIONS[r, p // M]) % M, TILES + 1 + r, p] = 1
    sel = np.concatenate([pick] * PARTS).astype(ml_dtypes.bfloat16)
    here_by = np.stack([0 * ROTATIONS[V], 0 * ROTATIONS[W], ROTATIONS[V], 0 * ROTATIONS[X]])
    there_by = ROTATIONS[[V, W, W, X]]
    assert sorted((there_by - here_by).ravel()) == list(range(1, 17)) and (there_by - here_by)[-1, -1] == 16
    here = (row + here_by[:, :, None]) % M
    there = (row + there_by[:, :, None]) % M
    w0 = f["L0_rec_W0"]
    as_w0 = lambda w: np.ascontiguousarray(w.reshape(TILES0, P, H).transpose(1, 0, 2))
    as_w = lambda w: np.ascontiguousarray(w.reshape(TILES, P, H).transpose(1, 0, 2))
    arrays = {
        "ids": f["ids"],
        "ctx_t": np.ascontiguousarray(f["dense_ctx"].T),
        **{f"tbl_{m}": f[f"tbl_{m}"] for m in range(M)},
        "sel": sel,
        "ident": np.eye(P, dtype=ml_dtypes.bfloat16),
        "w0a": as_w0(w0[here, there]),
        "w0b": as_w0(w0[there, here]),
        "w0d": np.ascontiguousarray(w0[row, row]),
        "w1": as_w(f["L0_rec_W1"]),
        "w2": as_w(f["L0_rec_W2"]),
        "wt1": f["W_top1"],
        "bt1": np.ascontiguousarray(f["b_top1"].reshape(F1 // P, P).T),
        "wt2": f["W_top2"],
        "bt2": np.ascontiguousarray(f["b_top2"].reshape(F2 // P, P).T),
        "wt3": np.ascontiguousarray(f["W_top3"].reshape(F2 // P, P).T),
    }
    nc = bacc.Bacc("TRN2", target_bir_lowering=False, num_devices=1)
    ap = {n: nc.dram_tensor(n, a.shape, mybir.dt.from_np(a.dtype), kind="ExternalInput").ap()
          for n, a in arrays.items()}
    out = nc.dram_tensor("y", (NT, P), F32, kind="ExternalOutput").ap()
    build(nc, ap["ids"], ap["ctx_t"], [ap[f"tbl_{m}"] for m in range(M)], ap["sel"], ap["ident"], ap["w0a"],
          ap["w0b"], ap["w0d"], ap["w1"], ap["w2"], ap["wt1"], ap["bt1"], ap["wt2"], ap["bt2"], ap["wt3"], out)
    r = run_bass_kernel_spmd(nc, [arrays], core_ids=[0])
    return r.results[0]["y"].reshape(B, 1)
```
